# Optimizing a Trainium2 kernel written in Bass

```python
import numpy as np
import jax
import jax.numpy as jnp

def _softmax(x, axis=-1):
    return jax.nn.softmax(x, axis=axis)

def _gelu(x):
    return jax.nn.gelu(x, approximate=True)

def _silu(x):
    return jax.nn.silu(x)

def _sigmoid(x):
    return jax.nn.sigmoid(x)

def _layernorm(x, axis=-1, eps=1e-05):
    m = jnp.mean(x, axis=axis, keepdims=True)
    v = jnp.var(x, axis=axis, keepdims=True)
    return (x - m) / jnp.sqrt(v + eps)

def _scatter_add(tgt, idx, src, axis=0):
    return tgt.at[idx].add(src)

def _segment_sum(src, seg, n):
    return jax.ops.segment_sum(src, seg, n)
kernel_name = 'mk_seq_preln_d1_jaxref_r8_3bf803'

def setup_inputs(seed: int=0):
    np.random.seed(seed)
    _w = jnp.asarray

    def _L0_attn_setup():
        import jax, jax.numpy as jnp
        import numpy as np
        D_MODEL = 128
        NUM_HEADS = 16
        D_K = D_MODEL // NUM_HEADS
        B, S = (4, 256)
        key = jax.random.key(seed)
        k1, k2, k3 = jax.random.split(key, 3)
        x = jax.random.normal(k1, (B, S, D_MODEL), dtype=jnp.float32)
        w_qkv = jax.random.normal(k2, (3, NUM_HEADS, D_K, D_MODEL), dtype=jnp.float32) / np.sqrt(D_MODEL)
        w_o = jax.random.normal(k3, (D_MODEL, D_MODEL), dtype=jnp.float32) / np.sqrt(D_MODEL)
        return {'x': x, 'w_qkv': w_qkv, 'w_o': w_o}
    _L0_attn_in = _L0_attn_setup()

    def _L0_ffn_setup():
        import jax, jax.numpy as jnp
        import numpy as np
        B, S, H, E, K = (2, 128, 128, 8, 2)
        F = 4 * H
        key = jax.random.key(seed)
        ks = jax.random.split(key, 8)
        std = 0.02
        return {'x': jax.random.normal(ks[0], (B, S, H), jnp.float32), 'gate_w': jax.random.normal(ks[1], (E, H), jnp.float32) * (std / np.sqrt(H)), 'gate_bias': jnp.zeros((E,), jnp.float32), 'Wu': jax.random.normal(ks[2], (E, F, H), jnp.float32) * std, 'bu': jnp.zeros((E, F), jnp.float32), 'Wd': jax.random.normal(ks[3], (E, H, F), jnp.float32) * std, 'bd': jnp.zeros((E, H), jnp.float32), 'sWu': jax.random.normal(ks[4], (F, H), jnp.float32) * std, 'sbu': jnp.zeros((F,), jnp.float32), 'sWd': jax.random.normal(ks[5], (H, F), jnp.float32) * std, 'sbd': jnp.zeros((H,), jnp.float32)}
    _L0_ffn_in = _L0_ffn_setup()
    _d = {'L0_attn_x': _L0_attn_in['x'], 'L0_attn_w_qkv': _L0_attn_in['w_qkv'], 'L0_attn_w_o': _L0_attn_in['w_o'], 'L0_ffn_gate_w': _L0_ffn_in['gate_w'], 'L0_ffn_gate_bias': _L0_ffn_in['gate_bias'], 'L0_ffn_Wu': _L0_ffn_in['Wu'], 'L0_ffn_bu': _L0_ffn_in['bu'], 'L0_ffn_Wd': _L0_ffn_in['Wd'], 'L0_ffn_bd': _L0_ffn_in['bd'], 'L0_ffn_sWu': _L0_ffn_in['sWu'], 'L0_ffn_sbu': _L0_ffn_in['sbu'], 'L0_ffn_sWd': _L0_ffn_in['sWd'], 'L0_ffn_sbd': _L0_ffn_in['sbd']}
    _x0 = _d['L0_attn_x']
    _d['L0_attn_x'] = jax.random.normal(jax.random.fold_in(jax.random.key(seed), 1), (8, 512, 128), dtype=_x0.dtype)
    del _x0
    return _d

def reference(L0_attn_x, L0_attn_w_qkv, L0_attn_w_o, L0_ffn_gate_w, L0_ffn_gate_bias, L0_ffn_Wu, L0_ffn_bu, L0_ffn_Wd, L0_ffn_bd, L0_ffn_sWu, L0_ffn_sbu, L0_ffn_sWd, L0_ffn_sbd):

    def _L0_attn_ref(x, w_qkv, w_o):
        import jax, jax.numpy as jnp
        import numpy as np
        D_MODEL = 128
        NUM_HEADS = 16
        D_K = D_MODEL // NUM_HEADS
        B, S = (4, 256)
        seq_len = x.shape[-2]
        d_k = w_qkv.shape[-2]
        qkv = jnp.einsum('bsm,qhkm->qbhsk', x, w_qkv)
        Q, K, V = (qkv[0], qkv[1], qkv[2])
        scores = jnp.einsum('bhsk,bhtk->bhst', Q, K) / jnp.sqrt(jnp.asarray(d_k, x.dtype))
        causal = jnp.tril(jnp.ones((seq_len, seq_len), dtype=bool))
        scores = jnp.where(causal, scores, -jnp.inf)
        probs = jax.nn.softmax(scores, axis=-1)
        attn = jnp.einsum('bhst,bhtk->bhsk', probs, V)
        b, h, s, k = attn.shape
        attn_cat = jnp.transpose(attn, (0, 2, 1, 3)).reshape(b, s, h * k)
        return jnp.einsum('bsd,md->bsm', attn_cat, w_o)

    def _L0_ffn_ref(x, gate_w, gate_bias, Wu, bu, Wd, bd, sWu, sbu, sWd, sbd):
        import jax, jax.numpy as jnp
        import numpy as np
        B, S, H, E, K = (2, 128, 128, 8, 2)
        F = 4 * H
        b, s, h = x.shape
        x_flat = x.reshape(-1, h)
        T = x_flat.shape[0]
        scores = jax.nn.sigmoid(x_flat @ gate_w.T + gate_bias)
        top_scores, top_idx = jax.lax.top_k(scores, K)
        top_scores = top_scores / (top_scores.sum(-1, keepdims=True) + 1e-06)
        w = jnp.zeros((T, E), x.dtype).at[jnp.arange(T)[:, None], top_idx].add(top_scores)
        h1 = jnp.einsum('th,efh->etf', x_flat, Wu) + bu[:, None, :]
        a1 = jax.nn.gelu(h1, approximate=False)
        y = jnp.einsum('etf,ehf->eth', a1, Wd) + bd[:, None, :]
        combined = jnp.einsum('te,eth->th', w, y)
        sh = jax.nn.gelu(x_flat @ sWu.T + sbu, approximate=False)
        shared = (sh @ sWd.T + sbd) * 0.1
        return (combined + shared).reshape(b, s, h)
    x = L0_attn_x
    x = x + _L0_attn_ref(_layernorm(x, axis=-1), L0_attn_w_qkv, L0_attn_w_o)
    x = x + _L0_ffn_ref(_layernorm(x, axis=-1), L0_ffn_gate_w, L0_ffn_gate_bias, L0_ffn_Wu, L0_ffn_bu, L0_ffn_Wd, L0_ffn_bd, L0_ffn_sWu, L0_ffn_sbu, L0_ffn_sWd, L0_ffn_sbd)
    return x

_drawn_inputs = setup_inputs


def setup_inputs(seed=0):
    import zlib

    import numpy as np

    out = dict(_drawn_inputs(seed))
    spreads = {'L0_ffn_gate_bias': (0.0, 0.1),
     'L0_ffn_bu': (0.0, 0.494),
     'L0_ffn_bd': (0.0, 0.1),
     'L0_ffn_sbu': (0.0, 0.8),
     'L0_ffn_sbd': (0.0, 0.8)}
    factors = {'L0_ffn_sWu': 8.0, 'L0_ffn_sWd': 8.0}
    for name, (base, spread) in spreads.items():
        noise = np.random.default_rng([zlib.crc32(name.encode()), seed]).standard_normal(out[name].shape)
        drawn = base * np.exp(spread * noise) if base else spread * noise
        out[name] = jnp.asarray(drawn.astype(out[name].dtype))
    for name, factor in factors.items():
        out[name] = (out[name] * factor).astype(out[name].dtype)
    return out
```

```python
import concourse.bass as bass
from concourse import mybir
from contextlib import ExitStack

FP32 = mybir.dt.float32
FP16 = mybir.dt.float16
BF16 = mybir.dt.bfloat16
U32 = mybir.dt.uint32
I32 = mybir.dt.int32
ALU = mybir.AluOpType
ACT = mybir.ActivationFunctionType
AX = mybir.AxisListType.X

P = 128
B, S, D = 8, 512, 128
H, DK = 16, 8
E, F = 8, 512
T = B * S
NT = T // P
QT = S // P
G, HG = 4, 4
FC = F // P
XS, WS, US, GS = 64.0, 64.0, 256.0, 4096.0
EPS = 1e-5
KTOP = 2
NX = 8
NJ = -(-((T * KTOP + E * (P - 1)) // P) // NX) * NX
NJB = NJ // NX
ROW = D + 1
NOWHERE = float(2 ** 30)

C_ID, C_CAUSAL, C_ONES, C_BEFORE, C_COL = 0, P, 2 * P, 3 * P, 4 * P
(K_SQ, K_SK, K_MASK, K_NEG, K_IOTA, K_POW, K_TILE) = (0, 1, 2, 6, 10, 18, 18 + NT)
C_WIDTH = C_COL + K_TILE + NJ


def constants():
    import numpy as np
    c = np.zeros((P, C_WIDTH), np.float32)
    p = np.arange(P)
    c[:, C_ID:C_ID + P] = np.eye(P)
    c[:, C_CAUSAL:C_CAUSAL + P] = np.where(p[:, None] >= p[None, :], 0.0, -1e30)
    c[0:3, C_ONES:C_ONES + P] = 1.0
    k = c[:, C_COL:]
    back = 1.0 / (XS * WS)
    k[:, K_SQ] = back * (p % 32 // DK == 2)
    k[:, K_SK] = back * (p % 32 // DK == 1)
    for j in range(HG):
        k[:, K_MASK + j] = (p // 32 == j)
        k[:, K_NEG + j] = -1.0 * (p == 32 * j + 3 * DK)
    c[:, C_BEFORE:C_BEFORE + P] = p[:, None] < p[None, :]
    k[:, K_IOTA:K_IOTA + E] = np.arange(E)
    k[:, K_POW:K_POW + NT] = -0.5
    k[:, K_TILE:K_TILE + NJ] = np.arange(NJ)
    return c


PAIR_UNITS = [[(0, 0, 0)], [(0, 1, 0), (0, 3, 384)], [(1, 0, 0)], [(1, 1, 0), (1, 3, 384)],
              [(0, 2, 0), (1, 2, 256)]]
UNITS = [[(2 * pair + h, t, c) for h, t, c in u] for pair in range(2) for u in PAIR_UNITS]
NU = len(UNITS)
WIDE = [(QT - t) * P for t in range(QT)]
PROB_AT = {(h, t): 512 * k + c for k, u in enumerate(PAIR_UNITS) for h, t, c in u}
REDS = [len(u) if len({t for _, t, _ in u}) > 1 else 1 for u in UNITS]
RED_TO = [sum(REDS[:u + 1]) for u in range(NU)]
NRED = RED_TO[-1]
SBANK = [i % 3 for i in range(G * NU)]
SBANK[-1] = 1


def before(i):
    j = i - 1
    while SBANK[j % (G * NU)] != SBANK[i]:
        j -= 1
    return j


def stages(b, g):
    if isinstance(b, int):
        s = 4 * b + g
        return [0 <= s - lag < B * G for lag in range(4)] + [g == 3 and b > 0]
    return [True] * 4 + [g == 3]


def blocks(eng, step):
    for g in range(G):
        step(0, g)
    with eng.Fori(1, B) as b:
        for g in range(G):
            step(b, g)
    for g in range(G):
        step(B, g)


PREP = 14
PE_ORDER = ([("a", 0), ("a", 1), ("b", 0), ("a", 2), ("b", 1), ("v", 0), ("a", 3), ("b", 2), ("a", 4), ("b", 3),
             ("a", 5), ("t", 0), ("w", 0), ("b", 4), ("a", 6), ("j", 0), ("b", 5), ("a", 7), ("b", 6), ("o", 0), ("a", 8), ("b", 7),
             ("a", 9), ("b", 8), ("b", 9), ("m", 0)])


def tile_blocks(eng, step, begin=None):
    for lo, hi in ((0, 1), (1, 2), (2, NJB), (NJB, NJB + 1)):
        if hi - lo == 1:
            extra = begin(lo) if begin else None
            for k in range(NX if lo < NJB else 2):
                step(lo, k, extra)
        else:
            with eng.Fori(lo, hi) as jb:
                extra = begin(jb) if begin else None
                for k in range(NX):
                    step(jb, k, extra)


def s_first(b, g, n):
    return isinstance(b, int) and 4 * b + g < n


def program(nc, x_d, wqkv_d, wo_d, gate_d, gbias_d, wu_d, bu_d, sbu_d, wd_d, bd_d, const_d, out_d):
    with ExitStack() as ctx:
        def sb(name, shape, dt=FP32):
            return ctx.enter_context(nc.sbuf_tensor(name, shape, dt))

        def sem(name):
            return ctx.enter_context(nc.semaphore(name))

        const = sb("const", [P, C_WIDTH])
        ident = const[:, C_ID:C_ID + P]
        identb = sb("identb", [P, P], BF16)
        causal = sb("causal", [P, P], BF16)
        onesb = sb("onesb", [P, P], BF16)

        def col(k, n=1):
            return const[:, C_COL + k:C_COL + k + n]

        x = sb("x", [P, NT, D])
        xn = sb("xn", [P, QT, D])
        x_hi = sb("x_hi", [P, T], FP16)
        x_lo = sb("x_lo", [P, T], FP16)
        stats = sb("stats", [P, NT, 6])
        mean, var, apart = sb("mean", [P, NT]), sb("var", [P, NT]), sb("apart", [P, NT])
        varc = sb("varc", [P, NT])
        rstd = sb("rstd", [P, NT])
        wqkv = sb("wqkv", [P, 3 * D])
        w_hi = sb("w_hi", [P, 3 * D], FP16)
        w_lo = sb("w_lo", [P, 3 * D], FP16)
        rep_hi = sb("rep_hi", [P, 2, H, 4, DK], FP16)
        rep_lo = sb("rep_lo", [P, 2, H, 4, DK], FP16)
        wo = sb("wo", [P, D])
        hi_q = sb("hi_q", [P, S], FP16)
        hi_k = sb("hi_k", [P, S], FP16)
        q4 = sb("q4", [P, 2, S], FP16)
        k4 = sb("k4", [P, 2, S], FP16)
        kh = sb("kh", [P, G, HG, S], FP16)
        qf = sb("qf", [P, 2, S], FP16)
        va = sb("va", [P, G, QT, HG, 32])
        mt = sb("mt", [P, 2, QT, P])
        pr = sb("pr", [P, 2, 2, 2560])
        ot = sb("ot", [P, S])
        rec = sb("rec", [P, QT, HG])
        attn = sb("attn", [P, QT, D])
        attn_t = sb("attn_t", [P, S])

        def bank(name):
            return ctx.enter_context(nc.psum_tensor(name, [P, 512], FP32))

        ps_a = [bank(f"ps_a{i}") for i in range(2)]
        ps_b = [bank(f"ps_b{i}") for i in range(3)]
        ps_o = bank("ps_o")
        ps_m = [bank(f"ps_m{i}") for i in range(2)]

        const_in, x_in, x_in2, w_in, out_done = (sem(n) for n in ("const_in", "x_in", "x_in2", "w_in", "out_done"))
        pool_passed, sp_passed = sem("pool_passed"), sem("sp_passed")
        prep, prep2, prep_act = sem("prep"), sem("prep2"), sem("prep_act")
        bn, mvr, varr, rstdr = sem("bn"), sem("mvr"), sem("varr"), sem("rstdr")
        xn_ready, xt_ready, xhi_ready, xlo_ready = sem("xn_ready"), sem("xt_ready"), sem("xhi_ready"), sem("xlo_ready")
        q_proj, k_proj, v_proj = sem("q_proj"), sem("k_proj"), sem("v_proj")
        a_unit, m_t, b_unit, pv_done, o_t = sem("a_unit"), sem("m_t"), sem("b_unit"), sem("pv_done"), sem("o_t")
        qhi_ready, khi_ready, v_ready, exped, o_out = sem("qhi_ready"), sem("khi_ready"), sem("v_ready"), sem("exped"), sem("o_out")
        q4_ready, k4_ready, maxed, qf_ready, rec_ready, normed = (
            sem(n) for n in ("q4_ready", "k4_ready", "maxed", "qf_ready", "rec_ready", "normed"))
        kh_ready, selected = sem("kh_ready"), sem("selected")
        at_t, at_out, wo_done, x2_ready = sem("at_t"), sem("at_out"), sem("wo_done"), sem("x2_ready")
        gate_done, topk = sem("gate_done"), sem("topk")
        wf_in, wprep = sem("wf_in"), sem("wprep")
        up_done, gelued, down_done, acced = sem("up_done"), sem("gelued"), sem("down_done"), sem("acced")

        NE = E + 1
        wu_hi = sb("wu_hi", [P, NE * F], FP16)
        wu_lo = sb("wu_lo", [P, NE * F], FP16)
        wu_raw = pr.rearrange("p a b c -> p (a b c)")[:, 0:NE * F]
        wd = sb("wd", [P, NE * FC * D])
        sbu = sb("sbu", [P, FC])
        gw = sb("gw", [P, E])
        gw_hi = sb("gw_hi", [P, E], FP16)
        gw_lo = sb("gw_lo", [P, E], FP16)
        gb = sb("gb", [P, E])
        NBU, NBD = E * F // P, NE * D // P
        bflat = sb("bflat", [P, NBU + NBD])
        bpart = sb("bpart", [P, 3, NBU + NBD], BF16)
        brest = sb("brest", [P, 2, NBU + NBD])
        bu_rows = sb("bu_rows", [P, E * F], BF16)
        bd_rows = sb("bd_rows", [P, NE * D], BF16)
        lg, sig = sb("lg", [P, NT, E]), sb("sig", [P, NT, E])
        top, idx, idf = sb("top", [P, NT, 8]), sb("idx", [P, NT, 8], U32), sb("idf", [P, NT, KTOP])
        oh, ohs = sb("oh", [P, KTOP, NT, E]), sb("ohs", [P, KTOP, NT, E])
        chosen = sb("chosen", [P, NT, E], BF16)
        beforeb, allb = sb("beforeb", [P, P], BF16), sb("allb", [P, P], BF16)
        sc, wgt, den = sb("sc", [P, KTOP, NT]), sb("wgt", [P, KTOP, NT]), sb("den", [P, NT])
        cum = sb("cum", [P, 2, NT, E])
        over, ends = sb("over", [P, E, NT]), sb("ends", [P, 4, E])
        posf, pos = sb("posf", [P, KTOP, NT]), sb("pos", [P, KTOP, NT], U32)
        past, te = sb("past", [P, NJ, E]), sb("te", [P, NJ])
        te_up, te_down = sb("te_up", [P, NJ + NX], I32), sb("te_down", [P, NJ + NX], I32)
        xr = pr.rearrange("p a b c -> p (a b c)")[:, 5120:5120 + NT * ROW].rearrange("p (t c) -> p t c", t=NT)
        blank = sb("blank", [P, ROW])
        ids = sb("ids", [P, KTOP, NT], I32)
        xt = sb("xt", [P, NX, ROW])
        xh, xl = sb("xh", [P, 2, P], FP16), sb("xl", [P, 2, P], FP16)
        ps_down = [ps_o, ps_b[2]]
        sh_bank = [ps_a[0], ps_a[1], ps_b[0], ps_b[1]]
        act2 = pr.rearrange("p a b c -> p (a b c)")[:, 4096:4096 + 2 * F]\
            .rearrange("p (a f s) -> p a f s", a=2, f=FC)
        act = kh.rearrange("p g h s -> p (g h s)").bitcast(FP32).rearrange("p (a f s) -> p a f s", a=2, f=FC)
        y = sb("y", [P, NX, D])
        yb = pr.rearrange("p a b c -> p (a b c)")[:, 0:2 * QT * KTOP * D]\
            .rearrange("p (a t k d) -> p a t k d", a=2, t=QT, k=KTOP)
        x_sorted = nc.dram_tensor("x_sorted", (NJ * P, ROW), FP32, kind="Internal").ap()
        y_token = nc.dram_tensor("y_token", (T * KTOP, D), FP32, kind="Internal").ap()
        blanked, rows_out, ids_set = sem("blanked"), sem("rows_out"), sem("ids_set")
        row_copied = sem("row_copied")
        bias_in, bias_split, bias_rows = sem("bias_in"), sem("bias_split"), sem("bias_rows")
        ranked, routed, chosen_ready = sem("ranked"), sem("routed"), sem("chosen_ready")
        sh_up, sh_act, sh_down, sh_added = sem("sh_up"), sem("sh_act"), sem("sh_down"), sem("sh_added")
        xt_in = [sem(f"xt_in{i}") for i in range(NX)]
        y_out = [sem(f"y_out{i}") for i in range(NX)]
        t_turned, t_hi, t_lo, t_up, t_act, t_down, t_y = (
            sem(n) for n in ("t_turned", "t_hi", "t_lo", "t_up", "t_act", "t_down", "t_y"))
        yb_in = [sem(f"yb_in{i}") for i in range(2)]
        summed, summed0 = sem("summed"), sem("summed0")

        block = ctx.enter_context(nc.Block())

        @block.sync
        def _(sp):
            sp.dma_start(const[:, :], const_d).then_inc(const_in, 16)
            xv = x_d.rearrange("(t p) d -> p t d", p=P)
            sp.dma_start(x[:, 0:QT, :], xv[:, 0:QT, :]).then_inc(x_in, 16)
            sp.dma_start(x[:, QT:NT, :], xv[:, QT:NT, :]).then_inc(x_in2, 16)
            sp.dma_start(wqkv[:, :], wqkv_d).then_inc(w_in, 16)
            sp.dma_start(wo[:, :], wo_d).then_inc(w_in, 16)
            sp.dma_start(gw[:, :], gate_d).then_inc(w_in, 16)
            sp.dma_start(gb[:, :], gbias_d.partition_broadcast(P)).then_inc(w_in, 16)
            sp.dma_start(wu_raw, wu_d).then_inc(wf_in, 16)
            sp.dma_start(wd[:, :], wd_d).then_inc(wf_in, 16)
            sp.dma_start(sbu[:, :], sbu_d).then_inc(wf_in, 16)
            sp.dma_start(bflat[:, 0:NBU], bu_d).then_inc(bias_in, 16)
            sp.dma_start(bflat[:, NBU:], bd_d).then_inc(bias_in, 16)
            sp.wait_ge(prep2, 7)
            sp.dma_start(x_sorted.rearrange("(j p) c -> p j c", p=P),
                         blank[:, :].unsqueeze(1).to_broadcast([P, NJ, ROW])).then_inc(blanked, 16)
            sp.wait_ge(bias_split, 6)
            sp.wait_ge(prep2, 9)
            for r in range(3):
                sp.dma_start(bu_rows[r:r + 1, :], bpart[:, r, 0:NBU]).then_inc(bias_rows, 16)
                sp.dma_start(bd_rows[r:r + 1, :], bpart[:, r, NBU:]).then_inc(bias_rows, 16)

            sp.wait_ge(rows_out, 16 * KTOP * NT)
            xs = x_sorted.rearrange("(j p) c -> p j c", p=P)

            def load(jb, k):
                j = NX * jb + k
                if not isinstance(jb, int):
                    sp.wait_ge(t_turned, j - NX + 1)
                    sp.sem_inc(sp_passed, 1)
                    sp.wait_ge(y_out[k], 16 * jb)
                    sp.sem_inc(sp_passed, 1)
                sp.dma_start(xt[:, k, :], xs[:, bass.ds(j, 1), :].rearrange("p a c -> p (a c)")).then_inc(xt_in[k], 16)

            for k in range(NX):
                load(0, k)
            with sp.Fori(1, NJB) as jb:
                for k in range(NX):
                    load(jb, k)

            for k in range(NX):
                sp.wait_ge(y_out[k], 16 * NJB)
            yv = y_token.rearrange("(t p k) d -> p t k d", p=P, k=KTOP)
            ov = out_d.rearrange("(t p) d -> p t d", p=P)

            def fetch(bp, i):
                for q in range(QT):
                    sp.dma_start(yb[:, i, q, :, :], yv[:, bass.ds((2 * bp + i) * QT + q, 1), :, :]
                                 .rearrange("p a k d -> p (a k) d")).then_inc(yb_in[i], 16)

            def send(bp, i):
                sp.wait_ge(summed, (2 * bp + i + 1) * QT)
                sp.sem_inc(sp_passed, 1)
                ts = bass.ds((2 * bp + i) * QT, QT)
                sp.dma_start(ov[:, ts, :], x[:, ts, :]).then_inc(out_done, 16)

            for i in range(2):
                fetch(0, i)
            with sp.Fori(1, B // 2) as bp:
                for i in range(2):
                    send(bp - 1, i)
                    fetch(bp, i)
            for i in range(2):
                send(B // 2 - 1, i)
            sp.wait_ge(out_done, 16 * B)

        @block.gpsimd
        def _(pool):
            nc.gpsimd.memset(va.rearrange("p g t h c -> p (g t h c)"), 0.0).then_inc(prep2, 1)
            pool.wait_ge(prep2, 1)
            nc.gpsimd.memset(va.rearrange("p g t h c -> p (g t h) c")[:, :, DK:DK + 1], 1.0).then_inc(prep2, 1)
            nc.gpsimd.memset(mt.rearrange("p a t c -> p (a t c)"), 0.0).then_inc(prep2, 1)
            nc.gpsimd.memset(rep_hi[:, :, :, 3, :], 0.0).then_inc(prep2, 1)
            nc.gpsimd.memset(rep_lo[:, :, :, 3, :], 0.0).then_inc(prep2, 1)

            nc.gpsimd.memset(blank[:, 0:D], 0.0).then_inc(prep2, 1)
            nc.gpsimd.iota(blank[:, D:ROW].bitcast(I32), pattern=[[0, 1]], base=int(NOWHERE), channel_multiplier=0)\
                .then_inc(prep2, 1)
            nc.gpsimd.memset(bu_rows[:, :], 0.0).then_inc(prep2, 1)
            nc.gpsimd.memset(bd_rows[:, :], 0.0).then_inc(prep2, 1)
            nc.gpsimd.memset(allb[:, :], 1.0).then_inc(prep2, 1)
            nc.gpsimd.iota(ids.rearrange("p k t -> p (k t)"), pattern=[[1, KTOP], [KTOP * P, NT]], base=0,
                           channel_multiplier=KTOP).then_inc(prep2, 1)

            def wait_alone(semaphore, value):
                pool.wait_ge(semaphore, value)
                pool.sem_inc(pool_passed, 1)

            def inverse_roots(n):
                pool.wait_ge(mvr, 6 * n)
                pool.wait_ge(const_in, 16)
                nc.gpsimd.tensor_scalar(varc[:, :], var[:, :], D * EPS, 1.0 / (D * XS * XS), ALU.add, ALU.mult)\
                    .then_inc(varr, 1)
                pool.wait_ge(varr, n)
                nc.gpsimd.tensor_tensor(rstd[:, :], varc[:, :], col(K_POW, NT), ALU.pow).then_inc(rstdr, 1)

            inverse_roots(1)

            def step(b, g):
                s = 4 * b + g
                project, _, scores, _, _ = stages(b, g)
                if project:
                    wait_alone(k4_ready, s + 1)
                    if not isinstance(b, int):
                        wait_alone(b_unit, (s - 3) * NU)
                    for j in range(HG):
                        nc.gpsimd.tensor_scalar(kh[:, g, j, :], k4[:, g % 2, :], col(K_MASK + j), col(K_NEG + j),
                                                ALU.mult, ALU.add).then_inc(kh_ready, 1)
                if scores:
                    n = s - 2
                    for pair in range(2):
                        row = pr[:, g % 2, pair, :]
                        wait_alone(exped, n * NU + 5 * (pair + 1))
                        for at, pattern in ((0, [[1024, 2], [512, 2], [1, P]]), (896, [[1024, 2], [1, P]]),
                                            (2048, [[256, 2], [1, P]])):
                            if len(pattern) == 3:
                                d = row[:, 0:2048].rearrange("p (a b c) -> p a b c", a=2, b=2)[:, :, :, 0:P]
                            elif at == 896:
                                d = row[:, 0:2048].rearrange("p (a c) -> p a c", a=2)[:, :, 896:1024]
                            else:
                                d = row[:, 2048:2560].rearrange("p (a c) -> p a c", a=2)[:, :, 0:P]
                            nc.gpsimd.affine_select(out=d, in_=d, pattern=[[0, k] for _, k in pattern[:-1]] + [[1, P]],
                                                    compare_op=ALU.is_ge, fill=0.0, base=0,
                                                    channel_multiplier=-1).then_inc(selected, 1)

            blocks(pool, step)
            inverse_roots(2)
            pool.wait_ge(blanked, 16)
            pool.wait_ge(prep2, 11)
            pool.wait_ge(row_copied, B)
            for k in range(KTOP):
                if k:
                    pool.wait_ge(rows_out, 16 * NT)
                nc.gpsimd.tensor_copy(xr[:, :, D].bitcast(I32), ids[:, k, :]).then_inc(ids_set, 1)
                pool.wait_ge(ids_set, k + 1)
                if not k:
                    pool.wait_ge(routed, 1)
                for t in range(NT):
                    nc.gpsimd.indirect_dma_start(x_sorted, bass.IndirectOffsetOnAxis(ap=pos[:, k, t:t + 1], axis=0),
                                                 xr[:, t, :], None).then_inc(rows_out, 16)

            def send(jb, k, _):
                if isinstance(jb, int) and not 0 <= NX * jb + k - 2 < NJ:
                    return
                j, q = NX * jb + k - 2, (k - 2) % NX
                wait_alone(t_y, j + 1)
                nc.gpsimd.indirect_dma_start(
                    y_token, bass.IndirectOffsetOnAxis(ap=xt[:, q, D:ROW].bitcast(U32), axis=0), y[:, q, :], None,
                    bounds_check=T * KTOP - 1, oob_is_err=False).then_inc(y_out[q], 16)

            tile_blocks(pool, send)

        @block.scalar
        def _(act_e):
            def hi_parts(base):
                with act_e.Fori(0, B) as b:
                    act_e.wait_ge(xt_ready, base + b + 1)
                    nc.scalar.activation(x_hi[:, bass.ds(b * S, S)], ps_m[0][:, :], ACT.Copy).then_inc(xhi_ready, 1)

            hi_parts(0)

            def step(b, g):
                s = 4 * b + g
                project, _, scores, values, output = stages(b, g)
                i0 = ((g - 2) % G) * NU

                def probs(units):
                    n = s - 2
                    for u in units:
                        act_e.wait_ge(b_unit, n * NU + u + 1)
                        if u == 0 and not (isinstance(b, int) and b == 0):
                            act_e.wait_ge(pv_done, n - 1)
                        pair, k = divmod(u, 5)
                        nc.scalar.activation(pr[:, g % 2, pair, 512 * k:512 * (k + 1)], ps_b[SBANK[i0 + u]][:, :],
                                             ACT.Exp, scale=float(DK) ** -0.5).then_inc(exped, 1)

                if project:
                    act_e.wait_ge(q_proj, s + 1)
                    if not (isinstance(b, int) and s == 0):
                        act_e.wait_ge(q4_ready, s)
                    nc.scalar.activation(hi_q[:, :], ps_m[0][:, :], ACT.Copy, scale=col(K_SQ)).then_inc(qhi_ready, 1)
                    act_e.wait_ge(k_proj, s + 1)
                    if not (isinstance(b, int) and s == 0):
                        act_e.wait_ge(k4_ready, s)
                    nc.scalar.activation(hi_k[:, :], ps_m[1][:, :], ACT.Copy, scale=col(K_SK)).then_inc(khi_ready, 1)
                if scores:
                    probs(range(0, 2))
                if project:
                    act_e.wait_ge(v_proj, s + 1)
                    if not isinstance(b, int):
                        act_e.wait_ge(pv_done, s - 3)
                    else:
                        act_e.wait_ge(prep2, 3)
                    nc.scalar.activation(va[:, g, :, :, 0:DK],
                                         ps_m[0][:, 0:P].rearrange("p (t h d) -> p t h d", t=QT, h=HG),
                                         ACT.Copy, scale=1.0 / (XS * WS)).then_inc(v_ready, 1)
                if scores:
                    probs(range(2, 4))
                if output:
                    act_e.wait_ge(at_t, b)
                    nc.scalar.activation(attn_t[:, :], ps_m[0][:, :], ACT.Copy).then_inc(at_out, 1)
                if scores:
                    probs(range(4, 6))
                if values:
                    n = s - 3
                    act_e.wait_ge(pv_done, n + 1)
                    if not (isinstance(b, int) and b == 0):
                        act_e.wait_ge(o_t, n)
                    nc.scalar.activation(ot[:, :], ps_o[:, :], ACT.Copy).then_inc(o_out, 1)
                if scores:
                    probs(range(6, 10))

            act_e.wait_ge(wprep, 2)
            blocks(act_e, step)
            with act_e.Fori(0, B) as b:
                act_e.wait_ge(xt_ready, B + b + 1)
                nc.scalar.activation(x_hi[:, bass.ds(b * S, S)], ps_m[0][:, :], ACT.Copy).then_inc(xhi_ready, 1)
                nc.scalar.activation(xr[:, bass.ds(b * QT, QT), 0:D], xn[:, :, :], ACT.Copy).then_inc(row_copied, 1)
            act_e.wait_ge(topk, 1)
            nc.scalar.activation(sig[:, :, :], lg[:, :, :], ACT.Exp, scale=-1.0).then_inc(prep_act, 1)
            act_e.wait_ge(wf_in, 48)
            with act_e.Fori(0, B) as b:
                for f in range(FC):
                    act_e.wait_ge(sh_up, FC * b + f + 1)
                    nc.scalar.activation(act[:, 0:2, :, :].rearrange("p a f s -> p (a f s)")[:, f * S:(f + 1) * S],
                                         sh_bank[f][:, :], ACT.Gelu, bias=sbu[:, f:f + 1], scale=1.0 / (XS * US))\
                        .then_inc(sh_act, 1)

            def tile_act(jb, k, _):
                j = NX * jb + k
                first = isinstance(jb, int) and jb == 0
                if not isinstance(jb, int) or j < NJ:
                    act_e.wait_ge(t_turned, j + 1)
                    if not (first and k < 2):
                        act_e.wait_ge(t_up, j - 1)
                    nc.scalar.activation(xh[:, k % 2, :], ps_m[k % 2][:, 0:P], ACT.Copy).then_inc(t_hi, 1)
                if not isinstance(jb, int) or 0 <= j - 1 < NJ:
                    act_e.wait_ge(t_up, j)
                    if not (first and k < 3):
                        act_e.wait_ge(t_down, j - 2)
                    nc.scalar.activation(act2[:, (k - 1) % 2, :, :].rearrange("p f s -> p (f s)"),
                                         ps_a[(k - 1) % 2][:, :], ACT.Gelu, scale=1.0 / (XS * US)).then_inc(t_act, 1)

            tile_blocks(act_e, tile_act)

        @block.vector
        def _(dve):
            v = nc.vector

            def statistics(first, last):
                with dve.Fori(first, last) as t:
                    v.bn_stats(stats[:, bass.ds(t, 1), :], x[:, bass.ds(t, 1), :]).then_inc(bn, 1)

            def mean_and_variance(n):
                dve.wait_ge(bn, n * NT)
                k = 6 * (n - 1)
                means, squares = (stats[:, :, c::3] for c in (1, 2))
                v.tensor_reduce(mean[:, :], means, AX, ALU.add).then_inc(mvr, 1)
                v.tensor_reduce(var[:, :], squares, AX, ALU.add).then_inc(mvr, 1)
                v.tensor_tensor(apart[:, :], stats[:, :, 1], stats[:, :, 4], ALU.subtract).then_inc(mvr, 1)
                dve.wait_ge(mvr, k + 3)
                v.tensor_scalar(mean[:, :], mean[:, :], 0.5, None, ALU.mult).then_inc(mvr, 1)
                v.scalar_tensor_tensor(apart[:, :], apart[:, :], D / 4.0, apart[:, :], ALU.mult, ALU.mult)\
                    .then_inc(mvr, 1)
                dve.wait_ge(mvr, k + 5)
                v.tensor_tensor(var[:, :], var[:, :], apart[:, :], ALU.add).then_inc(mvr, 1)

            def low_part(base, b):
                dve.wait_ge(xhi_ready, base + b + 1)
                v.tensor_tensor(x_lo[:, bass.ds(b * S, S)], ps_m[0][:, :], x_hi[:, bass.ds(b * S, S)],
                                ALU.subtract).then_inc(xlo_ready, 1)

            def normalise(base):
                with dve.Fori(0, B) as b:
                    for i in range(QT):
                        t = b * QT + i
                        v.tensor_scalar(xn[:, i, :], x[:, bass.ds(t, 1), :], mean[:, bass.ds(t, 1)],
                                        rstd[:, bass.ds(t, 1)], ALU.subtract, ALU.mult).then_inc(xn_ready, 1)
                    low_part(base, b)
                    if base:
                        dve.wait_ge(row_copied, b + 1)

            dve.wait_ge(x_in, 16)
            statistics(0, QT)
            dve.wait_ge(x_in2, 16)
            statistics(QT, NT)
            mean_and_variance(1)
            dve.wait_ge(bias_in, 32)
            v.tensor_scalar(bflat[:, 0:NBU], bflat[:, 0:NBU], XS * US, None, ALU.mult).then_inc(bias_split, 1)
            rest = bflat
            for r in range(3):
                dve.wait_ge(bias_split, 1 + 2 * r) if r else dve.wait_ge(bias_split, 1)
                v.tensor_copy(bpart[:, r, :], rest[:, :] if r == 0 else rest).then_inc(bias_split, 1)
                if r < 2:
                    dve.wait_ge(bias_split, 2 + 2 * r)
                    v.tensor_tensor(brest[:, r, :], rest[:, :] if r == 0 else rest, bpart[:, r, :], ALU.subtract)\
                        .then_inc(bias_split, 1)
                    rest = brest[:, r, :]
            dve.wait_ge(w_in, 64)
            dve.wait_ge(const_in, 16)
            v.tensor_scalar(w_hi[:, :], wqkv[:, :], WS, None, ALU.mult).then_inc(prep, 1)
            v.tensor_scalar(gw_hi[:, :], gw[:, :], GS, None, ALU.mult).then_inc(prep, 1)
            dve.wait_ge(prep, 2)
            v.scalar_tensor_tensor(w_lo[:, :], wqkv[:, :], WS, w_hi[:, :], ALU.mult, ALU.subtract).then_inc(prep, 1)
            v.scalar_tensor_tensor(gw_lo[:, :], gw[:, :], GS, gw_hi[:, :], ALU.mult, ALU.subtract).then_inc(prep, 1)
            dve.wait_ge(prep, 4)
            n = 4
            for src, dst in ((w_hi, rep_hi), (w_lo, rep_lo)):
                for r in range(3):
                    v.tensor_copy(dst[:, :, :, r, :], src[:, 0:2 * D].rearrange("p (a h d) -> p a h d", a=2, h=H))\
                        .then_inc(prep, 1)
            v.tensor_copy(identb[:, :], ident).then_inc(prep, 1)
            v.tensor_copy(causal[:, :], const[:, C_CAUSAL:C_CAUSAL + P]).then_inc(prep, 1)
            v.tensor_copy(onesb[:, :], const[:, C_ONES:C_ONES + P]).then_inc(prep, 1)
            v.tensor_copy(beforeb[:, :], const[:, C_BEFORE:C_BEFORE + P]).then_inc(prep, 1)
            dve.wait_ge(wf_in, 48)
            v.tensor_scalar(wu_hi[:, :], wu_raw, US, None, ALU.mult).then_inc(wprep, 1)
            dve.wait_ge(wprep, 1)
            v.scalar_tensor_tensor(wu_lo[:, :], wu_raw, US, wu_hi[:, :], ALU.mult, ALU.subtract).then_inc(wprep, 1)
            dve.wait_ge(rstdr, 1)
            normalise(0)

            def add_residual(b):
                dve.wait_ge(wo_done, b)
                xb = x[:, bass.ds((b - 1) * QT, QT), :].rearrange("p t d -> p (t d)")
                v.tensor_tensor(xb, ps_m[1][:, :], xb, ALU.add).then_inc(x2_ready, 1)

            def step(b, g):
                s = 4 * b + g
                project, maxima, _, values, output = stages(b, g)
                first = isinstance(b, int) and b == 0
                if project:
                    dve.wait_ge(qhi_ready, s + 1)
                    if not (first and g < 2):
                        dve.wait_ge(qf_ready, s - 1)
                    v.scalar_tensor_tensor(q4[:, g % 2, :], ps_m[0][:, :], 1.0 / (XS * WS), hi_q[:, :], ALU.mult,
                                           ALU.subtract).then_inc(q4_ready, 1)
                    dve.wait_ge(khi_ready, s + 1)
                    if not (first and g < 2):
                        dve.wait_ge(kh_ready, HG * (s - 1))
                    v.scalar_tensor_tensor(k4[:, g % 2, :], ps_m[1][:, :], 1.0 / (XS * WS), hi_k[:, :], ALU.mult,
                                           ALU.subtract).then_inc(k4_ready, 1)
                if maxima:
                    n = s - 1
                    par = (g - 1) % 2
                    for u in range(NU):
                        if output and u == 7:
                            add_residual(b)
                        dve.wait_ge(a_unit, n * NU + u + 1)
                        if u == 0 and not (first and g < 3):
                            dve.wait_ge(m_t, n - 1)
                        elif u == 0:
                            dve.wait_ge(prep2, 4)
                        src = ps_a[u % 2]
                        if REDS[u] == 1 and len(UNITS[u]) == 2:
                            h, t, _ = UNITS[u][0]
                            i = QT - 1 - t
                            at = 32 * h + 3 * DK
                            v.tensor_reduce(mt[:, par, i, at:at + 33:32],
                                            src[:, :].rearrange("p (a c) -> p a c", a=2), AX, ALU.max)\
                                .then_inc(maxed, 1)
                            continue
                        for h, t, c in UNITS[u]:
                            i = QT - 1 - t
                            at = 32 * h + 3 * DK
                            v.tensor_reduce(mt[:, par, i, at:at + 1], src[:, c:c + WIDE[t]], AX, ALU.max)\
                                .then_inc(maxed, 1)
                elif output:
                    add_residual(b)
                if values:
                    n = s - 3
                    gi = (g - 3) % G
                    dve.wait_ge(o_t, n + 1)
                    o = ps_m[0][:, :].rearrange("p (t h c) -> p t h c", t=QT, h=HG)
                    if not first:
                        dve.wait_ge(normed, n)
                    v.reciprocal(rec[:, :, :], o[:, :, :, DK]).then_inc(rec_ready, 1)
                    dve.wait_ge(rec_ready, n + 1)
                    out = attn[:, :, gi * 32:gi * 32 + 32].rearrange("p t (h d) -> p t h d", h=HG)
                    v.tensor_tensor(out, o[:, :, :, 0:DK],
                                    rec[:, :, :].unsqueeze(3).to_broadcast([P, QT, HG, DK]), ALU.mult)\
                        .then_inc(normed, 1)
                if maxima:
                    n = s - 1
                    par = (g - 1) % 2
                    dve.wait_ge(m_t, n + 1)
                    dve.wait_ge(q4_ready, n + 1)
                    if not (first and g < 3):
                        dve.wait_ge(b_unit, NU * (n - 1))
                    v.tensor_tensor(qf[:, par, :], q4[:, par, :], ps_m[1][:, :], ALU.add).then_inc(qf_ready, 1)

            blocks(dve, step)
            dve.wait_ge(x2_ready, B)
            dve.wait_ge(xn_ready, NT)
            dve.wait_ge(mvr, 6)
            statistics(0, NT)
            mean_and_variance(2)
            dve.wait_ge(rstdr, 2)
            normalise(B)
            count = [0]

            def then(ins):
                ins.then_inc(topk, 1)
                count[0] += 1
                dve.wait_ge(topk, count[0])

            def per_expert(ap):
                return ap.unsqueeze(1).to_broadcast([P, NT, E])

            dve.wait_ge(gate_done, B)
            logits = ps_m[1][:, 0:NT * E].rearrange("p (t e) -> p t e", e=E)
            then(v.scalar_tensor_tensor(lg[:, :, :], logits, 1.0 / (XS * GS), per_expert(gb[:, :]), ALU.mult, ALU.add))
            for t in range(NT):
                ins = v.max(top[:, t, :], lg[:, t, :])
            then(ins)
            for t in range(NT):
                ins = v.max_index(idx[:, t, :], top[:, t, :], lg[:, t, :])
            then(ins)
            then(v.tensor_copy(idf[:, :, :], idx[:, :, 0:KTOP]))
            for r in range(KTOP):
                ins = v.tensor_tensor(oh[:, r, :, :], idf[:, :, r].unsqueeze(2).to_broadcast([P, NT, E]),
                                      per_expert(col(K_IOTA, E)), ALU.is_equal)
            then(ins)
            v.tensor_tensor(chosen[:, :, :], oh[:, 0, :, :], oh[:, 1, :, :], ALU.add).then_inc(chosen_ready, 1)
            dve.wait_ge(ranked, 1)
            rank = ps_a[0][:, 0:NT * E].rearrange("p (t e) -> p t e", e=E)
            total = ps_a[0][:, NT * E:2 * NT * E].rearrange("p (t e) -> p t e", e=E)
            then(v.tensor_copy(cum[:, 0, :, :], total))
            a = 0
            step_t = 1
            while step_t < NT:
                v.tensor_copy(cum[:, 1 - a, 0:step_t, :], cum[:, a, 0:step_t, :]).then_inc(topk, 1)
                count[0] += 1
                then(v.tensor_tensor(cum[:, 1 - a, step_t:, :], cum[:, a, step_t:, :], cum[:, a, 0:NT - step_t, :],
                                     ALU.add))
                a, step_t = 1 - a, 2 * step_t
            then(v.scalar_tensor_tensor(over[:, :, :], cum[:, a, NT - 1, :].unsqueeze(2).to_broadcast([P, E, NT]),
                                        1.0 / P, col(K_TILE, NT).unsqueeze(1).to_broadcast([P, E, NT]), ALU.mult,
                                        ALU.is_gt))
            then(v.tensor_reduce(ends[:, 0, :], over[:, :, :], AX, ALU.add))
            then(v.tensor_copy(ends[:, 3, :], ends[:, 0, :]))
            c, step_e = 0, 1
            while step_e < E:
                v.tensor_copy(ends[:, 1 - c, 0:step_e], ends[:, c, 0:step_e]).then_inc(topk, 1)
                count[0] += 1
                then(v.tensor_tensor(ends[:, 1 - c, step_e:], ends[:, c, step_e:], ends[:, c, 0:E - step_e], ALU.add))
                c, step_e = 1 - c, 2 * step_e
            then(v.tensor_tensor(ends[:, 2, :], ends[:, c, :], ends[:, 3, :], ALU.subtract))
            then(v.tensor_scalar(ends[:, 3, :], ends[:, 2, :], float(P), None, ALU.mult))
            then(v.tensor_tensor(cum[:, a, :, :], cum[:, a, :, :], total, ALU.subtract))
            then(v.tensor_tensor(cum[:, a, :, :], cum[:, a, :, :], rank, ALU.add))
            then(v.tensor_tensor(cum[:, a, :, :], cum[:, a, :, :], per_expert(ends[:, 3, :]), ALU.add))
            for r in range(KTOP):
                ins = v.tensor_tensor(ohs[:, r, :, :], oh[:, r, :, :], cum[:, a, :, :], ALU.mult)
            then(ins)
            then(v.tensor_reduce(posf[:, :, :], ohs[:, :, :, :], AX, ALU.add))
            v.tensor_copy(pos[:, :, :], posf[:, :, :]).then_inc(routed, 1)
            then(v.tensor_tensor(past[:, :, :], col(K_TILE, NJ).unsqueeze(2).to_broadcast([P, NJ, E]),
                                 ends[:, c, :].unsqueeze(1).to_broadcast([P, NJ, E]), ALU.is_ge))
            then(v.tensor_reduce(te[:, :], past[:, :, :], AX, ALU.add))
            then(v.memset(te_up[:, :], 0))
            then(v.memset(te_down[:, :], 0))
            v.tensor_scalar(te_up[:, 1:1 + NJ], te[:, :], float(E - 1), None, ALU.min).then_inc(routed, 1)
            v.tensor_scalar(te_down[:, 2:2 + NJ], te[:, :], float(E - 1), None, ALU.min).then_inc(routed, 1)
            dve.wait_ge(prep_act, 1)
            then(v.tensor_scalar(sig[:, :, :], sig[:, :, :], 1.0, None, ALU.add))
            then(v.reciprocal(sig[:, :, :], sig[:, :, :]))
            for r in range(KTOP):
                ins = v.tensor_tensor(ohs[:, r, :, :], oh[:, r, :, :], sig[:, :, :], ALU.mult)
            then(ins)
            then(v.tensor_reduce(sc[:, :, :], ohs[:, :, :, :], AX, ALU.add))
            then(v.tensor_tensor(den[:, :], sc[:, 0, :], sc[:, 1, :], ALU.add))
            then(v.tensor_scalar(den[:, :], den[:, :], 1e-6, None, ALU.add))
            then(v.reciprocal(den[:, :], den[:, :]))
            then(v.tensor_tensor(wgt[:, :, :], sc[:, :, :], den[:, :].unsqueeze(1).to_broadcast([P, KTOP, NT]),
                                 ALU.mult))
            with dve.Fori(0, B) as b:
                dve.wait_ge(sh_down, b + 1)
                xb = x[:, bass.ds(b * QT, QT), :].rearrange("p t d -> p (t d)")
                v.scalar_tensor_tensor(xb, ps_o[:, :], 0.1, xb, ALU.mult, ALU.add).then_inc(sh_added, 1)

            def tile_parts(jb, k, _):
                j = NX * jb + k
                first = isinstance(jb, int) and jb == 0
                if not isinstance(jb, int) or j < NJ:
                    dve.wait_ge(t_hi, j + 1)
                    if not (first and k < 2):
                        dve.wait_ge(t_up, j - 1)
                    v.tensor_tensor(xl[:, k % 2, :], ps_m[k % 2][:, 0:P], xh[:, k % 2, :], ALU.subtract)\
                        .then_inc(t_lo, 1)
                if not isinstance(jb, int) or 0 <= j - 2 < NJ:
                    dve.wait_ge(t_down, j - 1)
                    q = (k - 2) % NX
                    sent = jb if k >= 2 else jb - 1
                    if not isinstance(jb, int) or sent > 0:
                        dve.wait_ge(y_out[q], 16 * sent)
                    v.tensor_copy(y[:, q, :], ps_down[k % 2][:, 0:D]).then_inc(t_y, 1)

            tile_blocks(dve, tile_parts)
            def add_experts(bp, i):
                m = 2 * bp + i
                dve.wait_ge(yb_in[i], 16 * QT * (bp + 1))
                for q in range(QT):
                    t = m * QT + q
                    xt1 = x[:, bass.ds(t, 1), :].rearrange("p a d -> p (a d)")
                    v.scalar_tensor_tensor(xt1, yb[:, i, q, 0, :], wgt[:, 0, bass.ds(t, 1)], xt1, ALU.mult, ALU.add)\
                        .then_inc(summed0, 1)
                for q in range(QT):
                    t = m * QT + q
                    xt1 = x[:, bass.ds(t, 1), :].rearrange("p a d -> p (a d)")
                    dve.wait_ge(summed0, t + 1)
                    v.scalar_tensor_tensor(xt1, yb[:, i, q, 1, :], wgt[:, 1, bass.ds(t, 1)], xt1, ALU.mult, ALU.add)\
                        .then_inc(summed, 1)

            with dve.Fori(0, B // 2) as bp:
                for i in range(2):
                    add_experts(bp, i)

        @block.tensor
        def _(pe):
            mm = nc.tensor.matmul

            def turned(base):
                with pe.Fori(0, B) as b:
                    pe.wait_ge(xn_ready, QT * (base + b + 1))
                    for i in range(QT):
                        last = nc.tensor.transpose(ps_m[0][:, i * P:(i + 1) * P], xn[:, i, :], ident)
                    last.then_inc(xt_ready, 1)
                    pe.wait_ge(xlo_ready, base + b + 1)


            pe.wait_ge(const_in, 16)
            turned(0)
            pe.wait_ge(prep, PREP)
            pe.wait_ge(prep2, 5)

            def project_q_k(b, g, s):
                xs = bass.ds(b * S, S)
                pe.wait_ge(xlo_ready, B)
                for a, ready, dst in ((0, q_proj, ps_m[0]), (1, k_proj, ps_m[1])):
                    if a == 0 and s_first(b, g, 4):
                        pe.wait_ge(v_ready, s) if not (isinstance(s, int) and s == 0) else None
                    elif a == 0:
                        pe.wait_ge(normed, s - 3)
                    elif s_first(b, g, 2):
                        pe.wait_ge(k4_ready, s) if not (isinstance(s, int) and s == 0) else None
                    else:
                        pe.wait_ge(qf_ready, s - 1)
                    hi = rep_hi[:, a, g * HG:(g + 1) * HG, :, :].rearrange("p h r d -> p (h r d)")
                    lo = rep_lo[:, a, g * HG:(g + 1) * HG, :, :].rearrange("p h r d -> p (h r d)")
                    mm(dst[:, :], hi, x_hi[:, xs], start=True, stop=False)
                    mm(dst[:, :], hi, x_lo[:, xs], start=False, stop=False)
                    mm(dst[:, :], lo, x_hi[:, xs], start=False, stop=True).then_inc(ready, 1)

            def project_v(b, g, s):
                pe.wait_ge(q4_ready, s + 1)
                cols = slice(2 * D + g * 32, 2 * D + (g + 1) * 32)
                for i in range(QT):
                    xs = bass.ds(b * S + i * P, P)
                    dst = ps_m[0][:, i * 32:(i + 1) * 32]
                    mm(dst, x_hi[:, xs], w_hi[:, cols], start=True, stop=False)
                    mm(dst, x_hi[:, xs], w_lo[:, cols], start=False, stop=False)
                    last = mm(dst, x_lo[:, xs], w_hi[:, cols], start=False, stop=True)
                last.then_inc(v_proj, 1)

            def step(b, g):
                s = 4 * b + g
                project, maxima, scores, values, output = stages(b, g)
                if project:
                    project_q_k(b, g, s)

                def a_scores(u):
                    n, gi, par = s - 1, (g - 1) % G, (g - 1) % 2
                    if u == 0:
                        pe.wait_ge(q4_ready, n + 1)
                        pe.wait_ge(kh_ready, HG * (n + 1))
                    if u >= 2:
                        pe.wait_ge(maxed, NRED * n + RED_TO[u - 2])
                    elif not s_first(b, g, 2):
                        pe.wait_ge(maxed, NRED * (n - 1) + RED_TO[u + NU - 2])
                    dst = ps_a[u % 2]
                    for h, t, c in UNITS[u]:
                        i = QT - 1 - t
                        w = WIDE[t]
                        mm(dst[:, c:c + w], q4[:, par, i * P:(i + 1) * P], kh[:, gi, h, 0:w], start=True, stop=False)
                        last = mm(dst[:, c + w - P:c + w], identb[:, :], causal[:, :], start=False, stop=True)
                    last.then_inc(a_unit, 1)

                def b_scores(u):
                    n, gi, par = s - 2, (g - 2) % G, g % 2
                    if u == 0:
                        pe.wait_ge(qf_ready, n + 1)
                    i0 = gi * NU + u
                    prev = before(i0)
                    if prev >= 0 or not (isinstance(b, int) and b == 0):
                        pe.wait_ge(exped, NU * (n - gi) + prev + 1)
                    dst = ps_b[SBANK[i0]]
                    for h, t, c in UNITS[u]:
                        last = mm(dst[:, c:c + WIDE[t]], kh[:, gi, h, t * P:(t + 1) * P], qf[:, par, t * P:S],
                                  start=True, stop=True)
                    last.then_inc(b_unit, 1)

                def weighted_values():
                    n, gi, par = s - 3, (g - 3) % G, (g - 3) % 2
                    pe.wait_ge(exped, NU * (n + 1))
                    pe.wait_ge(selected, 6 * (n + 1))
                    pe.wait_ge(v_ready, n + 1)
                    if not (isinstance(b, int) and b == 0):
                        pe.wait_ge(o_out, n)
                    for t in range(QT):
                        for h in range(HG):
                            at = PROB_AT[(h % 2, t)]
                            last = mm(ps_o[32 * h:32 * h + 32, t * P:S], va[:, gi, t, h, :],
                                      pr[:, par, h // 2, at:at + WIDE[t]], start=(t == 0), stop=(t == QT - 1))
                    last.then_inc(pv_done, 1)

                def outputs_turned():
                    n = s - 3
                    pe.wait_ge(o_out, n + 1)
                    if output:
                        pe.wait_ge(at_out, b)
                    elif project:
                        pe.wait_ge(v_ready, s + 1)
                    else:
                        pe.wait_ge(normed, n)
                    for i in range(QT):
                        last = nc.tensor.transpose(ps_m[0][:, i * P:(i + 1) * P], ot[:, i * P:(i + 1) * P], ident)
                    last.then_inc(o_t, 1)

                def attention_turned():
                    pe.wait_ge(normed, 4 * b)
                    if project:
                        pe.wait_ge(v_ready, s + 1)
                    for i in range(QT):
                        last = nc.tensor.transpose(ps_m[0][:, i * P:(i + 1) * P], attn[:, i, :], ident)
                    last.then_inc(at_t, 1)

                def output_projected():
                    pe.wait_ge(at_out, b)
                    pe.wait_ge(k4_ready, s + 1 if project else B * G)
                    for i in range(QT):
                        last = mm(ps_m[1][:, i * P:(i + 1) * P], attn_t[:, i * P:(i + 1) * P], wo[:, :], start=True,
                                  stop=True)
                    last.then_inc(wo_done, 1)

                def maxima_turned():
                    n, par = s - 1, (g - 1) % 2
                    pe.wait_ge(maxed, NRED * (n + 1))
                    if output:
                        pe.wait_ge(x2_ready, b)
                    elif project:
                        pe.wait_ge(k4_ready, s + 1)
                    else:
                        pe.wait_ge(qf_ready, n)
                    for i in range(QT):
                        last = nc.tensor.transpose(ps_m[1][:, i * P:(i + 1) * P], mt[:, par, i, :], ident)
                    last.then_inc(m_t, 1)

                for what, u in PE_ORDER:
                    if what == "a" and maxima:
                        a_scores(u)
                    elif what == "b" and scores:
                        b_scores(u)
                    elif what == "v" and project:
                        project_v(b, g, s)
                    elif what == "w" and values:
                        weighted_values()
                    elif what == "o" and values:
                        outputs_turned()
                    elif what == "t" and output:
                        attention_turned()
                    elif what == "j" and output:
                        output_projected()
                    elif what == "m" and maxima:
                        maxima_turned()

            blocks(pe, step)
            with pe.Fori(0, B) as b:
                pe.wait_ge(xn_ready, QT * (B + b + 1))
                for i in range(QT):
                    last = nc.tensor.transpose(ps_m[0][:, i * P:(i + 1) * P], xn[:, i, :], ident)
                last.then_inc(xt_ready, 1)
                pe.wait_ge(xlo_ready, B + b + 1)
                for i in range(QT):
                    xs = bass.ds(b * S + i * P, P)
                    dst = ps_m[1][:, bass.ds((b * QT + i) * E, E)]
                    mm(dst, x_hi[:, xs], gw_hi[:, :], start=True, stop=False)
                    mm(dst, x_hi[:, xs], gw_lo[:, :], start=False, stop=False)
                    last = mm(dst, x_lo[:, xs], gw_hi[:, :], start=False, stop=True)
                last.then_inc(gate_done, 1)
            pe.wait_ge(chosen_ready, 1)
            pe.wait_ge(prep2, 11)
            ch = chosen.rearrange("p t e -> p (t e)")
            mm(ps_a[0][:, 0:NT * E], beforeb[:, :], ch, start=True, stop=True)
            mm(ps_a[0][:, NT * E:2 * NT * E], allb[:, :], ch, start=True, stop=True).then_inc(ranked, 1)
            pe.wait_ge(wprep, 2)
            pe.wait_ge(wf_in, 48)
            pe.wait_ge(bias_rows, 96)
            pe.wait_ge(routed, 3)
            sact = act.rearrange("p a f s -> p (a f s)")
            with pe.Fori(0, B) as b:
                xs = bass.ds(b * S, S)
                for f in range(FC):
                    ws = slice(E * F + f * P, E * F + (f + 1) * P)
                    mm(sh_bank[f][:, :], wu_hi[:, ws], x_hi[:, xs], start=True, stop=False)
                    mm(sh_bank[f][:, :], wu_hi[:, ws], x_lo[:, xs], start=False, stop=False)
                    mm(sh_bank[f][:, :], wu_lo[:, ws], x_hi[:, xs], start=False, stop=True).then_inc(sh_up, 1)
                pe.wait_ge(sh_act, FC * (b + 1))
                for i in range(QT):
                    dst = ps_o[:, i * P:(i + 1) * P]
                    for f in range(FC):
                        ws = slice((E * FC + f) * D, (E * FC + f + 1) * D)
                        mm(dst, sact[:, f * S + i * P:f * S + (i + 1) * P], wd[:, ws], start=(f == 0), stop=False)
                    last = mm(dst, onesb[:, :], bd_rows[:, E * D:(E + 1) * D], start=False, stop=True)
                last.then_inc(sh_down, 1)
                pe.wait_ge(sh_added, b + 1)

            def numbers(table, jb):
                return nc.values_load_multi_w_load_instructions(
                    table[0:1, bass.ds(jb * NX, NX)], engines=[mybir.EngineType.PE], min_val=0, max_val=E - 1,
                    skip_runtime_bounds_check_because="an expert's number is below E by construction")[1]

            def experts(jb):
                up = numbers(te_up, jb)
                down = numbers(te_down, jb)
                return up, down

            def tile_mms(jb, k, e):
                j = NX * jb + k
                first = isinstance(jb, int) and jb == 0
                if not isinstance(jb, int) or j < NJ:
                    pe.wait_ge(xt_in[k], 16 * (jb + 1))
                    if not (first and k < 2):
                        pe.wait_ge(t_lo, j - 1)
                    nc.tensor.transpose(ps_m[k % 2][:, 0:P], xt[:, k, 0:D], ident).then_inc(t_turned, 1)
                if not isinstance(jb, int) or 0 <= j - 1 < NJ:
                    q = (k - 1) % 2
                    pe.wait_ge(t_lo, j)
                    if not (first and k < 3):
                        pe.wait_ge(t_act, j - 2)
                    for f in range(FC):
                        dst = ps_a[q][:, f * P:(f + 1) * P]
                        ws = bass.ds(e[0][k] * F + f * P, P)
                        mm(dst, wu_hi[:, ws], xh[:, q, :], start=True, stop=False)
                        mm(dst, wu_hi[:, ws], xl[:, q, :], start=False, stop=False)
                        mm(dst, wu_lo[:, ws], xh[:, q, :], start=False, stop=False)
                        last = mm(dst, bu_rows[:, ws], onesb[:, :], start=False, stop=True)
                    last.then_inc(t_up, 1)
                if not isinstance(jb, int) or 0 <= j - 2 < NJ:
                    q = k % 2
                    pe.wait_ge(t_act, j - 1)
                    if not (first and k < 4):
                        pe.wait_ge(t_y, j - 3)
                    for f in range(FC):
                        mm(ps_down[q][:, 0:D], act2[:, q, f, :], wd[:, bass.ds(e[1][k] * (FC * D) + f * D, D)],
                           start=(f == 0), stop=False)
                    mm(ps_down[q][:, 0:D], onesb[:, :], bd_rows[:, bass.ds(e[1][k] * D, D)], start=False, stop=True)\
                        .then_inc(t_down, 1)

            tile_blocks(pe, tile_mms, experts)


def kernel(L0_attn_x, L0_attn_w_qkv, L0_attn_w_o, L0_ffn_gate_w, L0_ffn_gate_bias, L0_ffn_Wu, L0_ffn_bu, L0_ffn_Wd,
           L0_ffn_bd, L0_ffn_sWu, L0_ffn_sbu, L0_ffn_sWd, L0_ffn_sbd):
    import numpy as np
    import concourse.bacc as bacc
    from concourse.bass_utils import run_bass_kernel_spmd

    a = {k: np.asarray(v) for k, v in locals().items() if k.startswith("L0_")}
    c = np.ascontiguousarray
    arrays = {
        "x": c(a["L0_attn_x"].reshape(T, D)),
        "wqkv": c(a["L0_attn_w_qkv"].reshape(3 * D, D).T),
        "wo": c(a["L0_attn_w_o"].T),
        "gate": c(a["L0_ffn_gate_w"].T),
        "gbias": c(a["L0_ffn_gate_bias"]),
        "wu": c(np.concatenate([a["L0_ffn_Wu"].reshape(E * F, D), a["L0_ffn_sWu"]]).T),
        "bu": c(a["L0_ffn_bu"].reshape(P, E * F // P)),
        "sbu": c(a["L0_ffn_sbu"].reshape(FC, P).T),
        "wd": c(np.concatenate([a["L0_ffn_Wd"], a["L0_ffn_sWd"][None]]).reshape(E + 1, D, FC, P)
                .transpose(3, 0, 2, 1).reshape(P, (E + 1) * FC * D)),
        "bd": c(np.concatenate([a["L0_ffn_bd"], a["L0_ffn_sbd"][None]]).reshape(P, (E + 1) * D // P)),
        "const": constants(),
    }
    nc = bacc.Bacc("TRN2", target_bir_lowering=False, num_devices=1)
    aps = [nc.dram_tensor(f"in_{k}", v.shape, FP32, kind="ExternalInput").ap() for k, v in arrays.items()]
    out = nc.dram_tensor("out", (T, D), FP32, kind="ExternalOutput").ap()
    program(nc, *aps, out)
    r = run_bass_kernel_spmd(nc, [{f"in_{k}": v for k, v in arrays.items()}], core_ids=[0])
    return r.results[0]["out"].reshape(B, S, D)
```

```python
import concourse.bass as bass
from concourse import mybir
from contextlib import ExitStack

FP32 = mybir.dt.float32
FP16 = mybir.dt.float16
BF16 = mybir.dt.bfloat16
U32 = mybir.dt.uint32
I32 = mybir.dt.int32
ALU = mybir.AluOpType
ACT = mybir.ActivationFunctionType
AX = mybir.AxisListType.X

P = 128
B, S, D = 8, 512, 128
H, DK = 16, 8
E, F = 8, 512
T = B * S
NT = T // P
QT = S // P
G, HG = 4, 4
FC = F // P
XS, WS, US, GS = 64.0, 64.0, 256.0, 4096.0
EPS = 1e-5
KTOP = 2
PARTS = 2
TP, NTP = T // PARTS, NT // PARTS
NX = 8
NJBP = -(-((TP * KTOP + E * (P - 1)) // P) // NX)
NJP, NJB = NJBP * NX, PARTS * NJBP
NJ = NJB * NX
BP = B // PARTS
assert BP < NJBP
COMBINE = 4
ROW = D + 1
NOWHERE = float(2 ** 30)

C_ID, C_CAUSAL, C_ONES, C_BEFORE, C_COL = 0, P, 2 * P, 3 * P, 4 * P
K_SQ, K_SK, K_MASK, K_NEG, K_REV = 0, 1, 2, 2 + HG, 2 + 2 * HG
K_POW = K_REV + E
K_TILE = K_POW + QT
K_ENDS = K_TILE + NJP
K_ROW = K_ENDS + 2 * E * E
C_WIDTH = C_COL + K_ROW + 3


def constants():
    import numpy as np
    c = np.zeros((P, C_WIDTH), np.float32)
    p = np.arange(P)
    c[:, C_ID:C_ID + P] = np.eye(P)
    c[:, C_CAUSAL:C_CAUSAL + P] = np.where(p[:, None] >= p[None, :], 0.0, -1e30)
    c[0:3, C_ONES:C_ONES + P] = 1.0
    k = c[:, C_COL:]
    back = 1.0 / (XS * WS)
    k[:, K_SQ] = back * (p % 32 // DK == 2)
    k[:, K_SK] = back * (p % 32 // DK == 1)
    for j in range(HG):
        k[:, K_MASK + j] = (p // 32 == j)
        k[:, K_NEG + j] = -1.0 * (p == 32 * j + 3 * DK)
    c[:, C_BEFORE:C_BEFORE + P] = p[:, None] < p[None, :]
    k[:, K_REV:K_REV + E] = E - np.arange(E)
    k[:, K_POW:K_POW + QT] = -0.5
    k[:, K_TILE:K_TILE + NJP] = np.arange(NJP)
    for r in range(3):
        k[r, K_ROW + r] = 1.0
    f, e = np.arange(E)[None, :], np.arange(E)[:, None]
    k[:, K_ENDS:K_ENDS + 2 * E * E] = np.stack([f <= e, P * (f < e)]).reshape(1, -1)
    return c


PAIR_UNITS = [[(0, 0, 0)], [(0, 1, 0), (0, 3, 384)], [(1, 0, 0)], [(1, 1, 0), (1, 3, 384)],
              [(0, 2, 0), (1, 2, 256)]]
UNITS = [[(2 * pair + h, t, c) for h, t, c in u] for pair in range(2) for u in PAIR_UNITS]
NU = len(UNITS)
WIDE = [(QT - t) * P for t in range(QT)]
PROB_AT = {(h, t): 512 * k + c for k, u in enumerate(PAIR_UNITS) for h, t, c in u}
REDS = [len(u) if len({t for _, t, _ in u}) > 1 else 1 for u in UNITS]
RED_TO = [sum(REDS[:u + 1]) for u in range(NU)]
NRED = RED_TO[-1]
SBANK = [i % 3 for i in range(G * NU)]
SBANK[-1] = 1


def before(i):
    j = i - 1
    while SBANK[j % (G * NU)] != SBANK[i]:
        j -= 1
    return j


def stages(b, g):
    if isinstance(b, int):
        s = 4 * b + g
        return [0 <= s - lag < B * G for lag in range(4)] + [g == 3 and b > 0]
    return [True] * 4 + [g == 3]


def blocks(eng, step):
    for b in (0, 1):
        for g in range(G):
            step(b, g)
    with eng.Fori(2, B - 1) as b:
        for g in range(G):
            step(b, g)
    for b in (B - 1, B):
        for g in range(G):
            step(b, g)


def early(b, g, n):
    return isinstance(b, int) and 4 * b + g < n


def normalisations(b, g):
    has = [not isinstance(b, int) or b + 1 < B, not isinstance(b, int) or b >= 2]
    taken = {0: 1, 1: 0}.get(g)
    turned = {1: 1, 2: 0}.get(g)
    return [k if k is not None and has[k] else None for k in (taken, turned)]


def normalised(kind, b):
    return b + 1 if kind == 0 else b - 2


PREP = 10
PE_ORDER = [("q", 0), ("a", 0), ("m", 0), ("a", 1), ("a", 2), ("w", 0), ("b", 0), ("k", 0), ("a", 3), ("b", 1),
            ("a", 4), ("b", 2), ("w", 1), ("b", 3), ("w", 2), ("a", 5), ("t", 0), ("a", 6), ("b", 4), ("w", 3),
            ("j", 0), ("v", 0), ("a", 7), ("b", 5), ("x", 0), ("b", 6), ("o", 0), ("a", 8), ("b", 7), ("b", 8),
            ("a", 9), ("b", 9)]

ACT_ORDER = [("q", 0), ("k", 0), ("e", 0), ("e", 1), ("e", 2), ("e", 3), ("t", 0), ("e", 4), ("o", 0), ("v", 0),
             ("e", 5), ("e", 6), ("h", 0), ("e", 7), ("e", 8), ("e", 9), ("c", 0)]

DVE_ORDER = [("r", 0), ("f", 0), ("r", 1), ("y", 0), ("r", 2), ("q", 0), ("r", 3), ("r", 4), ("k", 0), ("s", 0),
             ("r", 5), ("r", 6), ("x", 0), ("r", 7), ("n", 0), ("l", 0), ("r", 8), ("r", 9)]


def tile_blocks(eng, step, begin=None):
    for lo, hi in ((0, 1), (1, 2), (2, NJBP), (NJBP, NJBP + 1), (NJBP + 1, NJB), (NJB, NJB + 1)):
        if hi - lo == 1:
            extra = begin(lo) if begin else None
            for k in range(NX if lo < NJB else 2):
                step(lo, k, extra, lo // NJBP)
        else:
            with eng.Fori(lo, hi) as jb:
                extra = begin(jb) if begin else None
                for k in range(NX):
                    step(jb, k, extra, lo // NJBP)


def program(nc, x_d, wqkv_d, wo_d, gate_d, gbias_d, wu_d, bu_d, sbu_d, wd_d, bd_d, const_d, out_d):
    with ExitStack() as ctx:
        def sb(name, shape, dt=FP32):
            return ctx.enter_context(nc.sbuf_tensor(name, shape, dt))

        def sem(name):
            return ctx.enter_context(nc.semaphore(name))

        const = sb("const", [P, C_WIDTH])
        ident = const[:, C_ID:C_ID + P]
        identb = sb("identb", [P, P], BF16)
        causal = sb("causal", [P, P], BF16)
        onesb = sb("onesb", [P, P], BF16)

        def col(k, n=1):
            return const[:, C_COL + k:C_COL + k + n]

        x = sb("x", [P, NT, D])
        xn = sb("xn", [P, 2, QT, D])
        x_hi = sb("x_hi", [P, T], FP16)
        x_lo = sb("x_lo", [P, T], FP16)
        stats, mv = sb("stats", [P, 2, QT, 6]), sb("mv", [P, 2, QT, 2])
        varc, rstd = sb("varc", [P, 2, QT]), sb("rstd", [P, 2, QT])
        wqkv = sb("wqkv", [P, 3 * D])
        w_hi = sb("w_hi", [P, 3 * D], FP16)
        w_lo = sb("w_lo", [P, 3 * D], FP16)
        rep_hi = sb("rep_hi", [P, 2, H, 4, DK], FP16)
        rep_lo = sb("rep_lo", [P, 2, H, 4, DK], FP16)
        wo = sb("wo", [P, D])
        hi_q = sb("hi_q", [P, S], FP16)
        hi_k = sb("hi_k", [P, S], FP16)
        q4 = sb("q4", [P, 2, S], FP16)
        k4 = sb("k4", [P, 2, S], FP16)
        kh = sb("kh", [P, G, HG, S], FP16)
        qf = sb("qf", [P, 2, S], FP16)
        va = sb("va", [P, QT, G, HG, 32])
        mt = sb("mt", [P, 2, QT, P])
        pr = sb("pr", [P, 2, 2, 2560])
        ot = sb("ot", [P, S])
        rec = sb("rec", [P, QT, HG])
        attn = sb("attn", [P, QT, D])
        attn_t = sb("attn_t", [P, S])

        spare = pr.rearrange("p a b c -> p (a b c)")
        spare_at = [0]

        def in_spare(*shape):
            n = 1
            for k in shape:
                n *= k
            spare_at[0] += n
            flat = spare[:, spare_at[0] - n:spare_at[0]]
            names = "abcd"[:len(shape)]
            return flat.rearrange(f"p ({' '.join(names)}) -> p {' '.join(names)}", **dict(zip(names, shape)))

        def bank(name):
            return ctx.enter_context(nc.psum_tensor(name, [P, 512], FP32))

        ps_a = [bank(f"ps_a{i}") for i in range(2)]
        ps_b = [bank(f"ps_b{i}") for i in range(3)]
        ps_o = bank("ps_o")
        ps_m = [bank(f"ps_m{i}") for i in range(2)]

        const_in, x_in, x_in2, w_in, out_done = (sem(n) for n in ("const_in", "x_in", "x_in2", "w_in", "out_done"))
        pool_passed, sp_passed, rep_zeroed = sem("pool_passed"), sem("sp_passed"), sem("rep_zeroed")
        dve_passed, wqkv_in = sem("dve_passed"), sem("wqkv_in")
        prep, prep2 = sem("prep"), sem("prep2")
        bn_ready, mv_ready, var_ready, rstd_ready, xn_ready, xt_ready, xhi_ready, xlo_ready = (
            [sem(f"{n}{k}") for k in range(2)] for n in (
                "bn_ready", "mv_ready", "var_ready", "rstd_ready", "xn_ready", "xt_ready", "xhi_ready", "xlo_ready"))
        q_proj, k_proj, v_proj = sem("q_proj"), sem("k_proj"), sem("v_proj")
        a_unit, m_t, b_unit, pv_done, o_t = sem("a_unit"), sem("m_t"), sem("b_unit"), sem("pv_done"), sem("o_t")
        qhi_ready, khi_ready, v_ready, exped, o_out = sem("qhi_ready"), sem("khi_ready"), sem("v_ready"), sem("exped"), sem("o_out")
        q4_ready, k4_ready, maxed, qf_ready, rec_ready, normed = (
            sem(n) for n in ("q4_ready", "k4_ready", "maxed", "qf_ready", "rec_ready", "normed"))
        kh_ready, selected = sem("kh_ready"), sem("selected")
        at_t, at_out, wo_done, x2_ready = sem("at_t"), sem("at_out"), sem("wo_done"), sem("x2_ready")
        gate_done, logits_ready, exp_ready, topk = (
            sem(n) for n in ("gate_done", "logits_ready", "exp_ready", "topk"))
        wf_in, wu_high, wu_low, ffn_prep = (sem(n) for n in ("wf_in", "wu_high", "wu_low", "ffn_prep"))

        NE = E + 1
        wu_hi = sb("wu_hi", [P, NE * F], FP16)
        wu_lo = sb("wu_lo", [P, NE * F], FP16)
        wu_raw = sb("wu_raw", [P, NE * F])
        xr = wu_raw[:, 0:NT * ROW].rearrange("p (t c) -> p t c", t=NT)
        wd = sb("wd", [P, NE * FC * D])
        sbu = sb("sbu", [P, FC])
        gw = sb("gw", [P, E])
        gw_hi = sb("gw_hi", [P, E], FP16)
        gw_lo = sb("gw_lo", [P, E], FP16)
        gb = sb("gb", [P, E])
        bu = sb("bu", [P, E * FC])
        bd = sb("bd", [P, NE * D])
        bpart = sb("bpart", [P, 3, D], BF16)
        brest = sb("brest", [P, 2, D])
        bd_rows = sb("bd_rows", [P, D], BF16)
        lg, sig = in_spare(NT, E), in_spare(NT, E)
        score, key, rest_of = sb("score", [P, KTOP, NT]), sb("key", [P, KTOP, NT]), in_spare(NTP, E)
        tied = in_spare(NTP, E)
        oh, ohs = in_spare(PARTS, KTOP, NTP, E), in_spare(KTOP, NTP, E)
        chosen = sb("chosen", [P, NT, E], BF16)
        beforeb, allb = sb("beforeb", [P, P], BF16), sb("allb", [P, P], BF16)
        wgt, den = sb("wgt", [P, KTOP, NT]), sb("den", [P, NT])
        over, tiles, ends = in_spare(E, NTP), sb("tiles", [P, E]), sb("ends", [P, 2, E])
        share, place = in_spare(2, E, E), in_spare(NTP, E)
        posf, pos = sb("posf", [P, PARTS, KTOP, NTP]), sb("pos", [P, PARTS, KTOP, NTP], U32)
        past, te = in_spare(NJP, E), sb("te", [P, NJP])
        te_up, te_down = sb("te_up", [P, NJ + NX], I32), sb("te_down", [P, NJ + NX], I32)
        blank = sb("blank", [P, ROW])
        ids = sb("ids", [P, KTOP, NTP], I32)
        xt = in_spare(NX, ROW)
        xh, xl = sb("xh", [P, 2, P], FP16), sb("xl", [P, 2, P], FP16)
        ps_down = [ps_o, ps_b[2]]
        sh_bank = [ps_a[0], ps_a[1], ps_b[0], ps_b[1]]
        act2 = in_spare(2, FC, P)
        act = kh.rearrange("p g h s -> p (g h s)").bitcast(FP32).rearrange("p (a f s) -> p a f s", a=2, f=FC)
        y = in_spare(NX, D)
        yb = in_spare(BP, QT, KTOP, D)
        x_sorted = [nc.dram_tensor(f"x_sorted{h}", (NJP * P, ROW), FP32, kind="Internal").ap() for h in range(PARTS)]
        y_token = [nc.dram_tensor(f"y_token{h}", (TP * KTOP, D), FP32, kind="Internal").ap() for h in range(PARTS)]
        blanked, ids_set = sem("blanked"), sem("ids_set")
        rows_out = [sem(f"rows_out{h}") for h in range(PARTS)]
        row_copied = sem("row_copied")
        bias_in, bias_split = sem("bias_in"), sem("bias_split")
        ranked, routed, chosen_ready = sem("ranked"), sem("routed"), sem("chosen_ready")
        sh_up, sh_act, sh_down, sh_added = sem("sh_up"), sem("sh_act"), sem("sh_down"), sem("sh_added")
        xt_in = [sem(f"xt_in{i}") for i in range(NX)]
        y_out = [sem(f"y_out{i}") for i in range(NX)]
        t_turned, t_hi, t_lo, t_up, t_act, t_down, t_y = (
            sem(n) for n in ("t_turned", "t_hi", "t_lo", "t_up", "t_act", "t_down", "t_y"))
        yb_in, yb_in_last = sem("yb_in"), [sem(f"yb_in_last{i}") for i in range(BP)]
        tables_ready = sem("tables_ready")
        summed, summed0 = sem("summed"), sem("summed0")

        def numbers(table, jb, engine):
            return nc.values_load_multi_w_load_instructions(
                table[0:1, bass.ds(jb * NX, NX)], engines=[engine], min_val=0, max_val=E - 1,
                skip_runtime_bounds_check_because="an expert's number is below E by construction")[1]

        block = ctx.enter_context(nc.Block())

        @block.sync
        def _(sp):
            xv = x_d.rearrange("(t p) d -> p t d", p=P)
            sp.dma_start(x[:, 0:QT, :], xv[:, 0:QT, :]).then_inc(x_in, 16)
            sp.dma_start(const[:, :], const_d).then_inc(const_in, 16)
            sp.dma_start(wqkv[:, :], wqkv_d).then_inc(wqkv_in, 16)
            sp.dma_start(x[:, QT:NT, :], xv[:, QT:NT, :]).then_inc(x_in2, 16)
            sp.dma_start(wo[:, :], wo_d).then_inc(w_in, 16)
            sp.dma_start(gw[:, :], gate_d).then_inc(w_in, 16)
            sp.dma_start(gb[:, :], gbias_d.partition_broadcast(P)).then_inc(w_in, 16)
            sp.dma_start(wu_raw[:, :], wu_d).then_inc(wf_in, 16)
            sp.dma_start(wd[:, :], wd_d).then_inc(wf_in, 16)
            sp.dma_start(sbu[:, :], sbu_d).then_inc(wf_in, 16)
            sp.dma_start(bu[:, :], bu_d).then_inc(bias_in, 16)
            sp.dma_start(bd[:, :], bd_d.partition_broadcast(P)).then_inc(bias_in, 16)
            sp.wait_ge(prep2, 5)
            for h in range(PARTS):
                sp.dma_start(x_sorted[h].rearrange("(j p) c -> p j c", p=P),
                             blank[:, :].unsqueeze(1).to_broadcast([P, NJP, ROW])).then_inc(blanked, 16)
            xs = [x_sorted[h].rearrange("(j p) c -> p j c", p=P) for h in range(PARTS)]
            yv = [y_token[h].rearrange("(t p k) d -> p t k d", p=P, k=KTOP) for h in range(PARTS)]
            ov = out_d.rearrange("(t p) d -> p t d", p=P)

            def load(jb, k, h):
                j = NX * jb + k
                if not (isinstance(jb, int) and jb == 0):
                    sp.wait_ge(t_turned, j - NX + 1)
                    sp.sem_inc(sp_passed, 1)
                    sp.wait_ge(y_out[k], 16 * jb)
                    sp.sem_inc(sp_passed, 1)
                sp.dma_start(xt[:, k, :], xs[h][:, bass.ds(j - h * NJP, 1), :].rearrange("p a c -> p (a c)"))\
                    .then_inc(xt_in[k], 16)

            def fetch(h, batch, i, ready):
                for q in range(QT):
                    sp.dma_start(yb[:, i, q, :, :], yv[h][:, bass.ds(batch * QT + q, 1), :, :]
                                 .rearrange("p a k d -> p (a k) d")).then_inc(ready, 16)

            sp.wait_ge(rows_out[0], 16 * KTOP * NTP)
            for k in range(NX):
                load(0, k, 0)
            with sp.Fori(1, NJBP) as jb:
                for k in range(NX):
                    load(jb, k, 0)
            sp.wait_ge(rows_out[1], 16 * KTOP * NTP)
            for k in range(NX):
                load(NJBP, k, 1)
            with sp.Fori(NJBP + 1, NJBP + 1 + BP) as jb:
                for k in range(NX):
                    load(jb, k, 1)
                    if k == COMBINE + QT - NX // 2:
                        sp.wait_ge(summed, (jb - NJBP) * QT)
                        sp.sem_inc(sp_passed, 1)
                        fetch(0, jb - (NJBP + 1), 0, yb_in)
            for k in range(NX):
                sp.wait_ge(y_out[k], 16 * NJB)
            for i in range(BP):
                fetch(1, i, i, yb_in_last[i])
            sp.wait_ge(summed, (BP + 1) * QT)
            sp.dma_start(ov[:, 0:NTP, :], x[:, 0:NTP, :]).then_inc(out_done, 16)
            for i in range(BP):
                sp.wait_ge(summed, (BP + 2 + i) * QT)
                ts = slice(NTP + i * QT, NTP + (i + 1) * QT)
                sp.dma_start(ov[:, ts, :], x[:, ts, :]).then_inc(out_done, 16)
            sp.wait_ge(out_done, 16 * (BP + 1))

        @block.gpsimd
        def _(pool):
            def wait_alone(semaphore, value):
                pool.wait_ge(semaphore, value)
                pool.sem_inc(pool_passed, 1)

            nc.gpsimd.memset(rep_hi[:, :, :, 3, :], 0.0).then_inc(rep_zeroed, 1)
            nc.gpsimd.memset(rep_lo[:, :, :, 3, :], 0.0).then_inc(rep_zeroed, 1)

            def inverse_roots(kind, batch):
                n = batch + 1
                wait_alone(mv_ready[kind], QT * n)
                nc.gpsimd.tensor_scalar(varc[:, kind, :], mv[:, kind, :, 1], EPS, 1.0 / (XS * XS), ALU.add, ALU.mult)\
                    .then_inc(var_ready[kind], 1)
                wait_alone(var_ready[kind], n)
                nc.gpsimd.tensor_tensor(rstd[:, kind, :], varc[:, kind, :], col(K_POW, QT), ALU.pow)\
                    .then_inc(rstd_ready[kind], 1)

            pool.wait_ge(const_in, 16)
            inverse_roots(0, 0)

            nc.gpsimd.memset(mt.rearrange("p a t c -> p (a t c)"), 0.0).then_inc(prep2, 1)
            nc.gpsimd.memset(va.rearrange("p t g h c -> p (t g h c)"), 0.0).then_inc(prep2, 1)
            pool.wait_ge(prep2, 2)
            nc.gpsimd.memset(va.rearrange("p t g h c -> p (t g h) c")[:, :, DK:DK + 1], 1.0).then_inc(prep2, 1)
            nc.gpsimd.memset(blank[:, 0:D], 0.0).then_inc(prep2, 1)
            nc.gpsimd.iota(blank[:, D:ROW].bitcast(I32), pattern=[[0, 1]], base=int(NOWHERE), channel_multiplier=0)\
                .then_inc(prep2, 1)
            nc.gpsimd.memset(allb[:, :], 1.0).then_inc(prep2, 1)
            nc.gpsimd.iota(ids.rearrange("p k t -> p (k t)"), pattern=[[1, KTOP], [KTOP * P, NTP]], base=0,
                           channel_multiplier=KTOP).then_inc(prep2, 1)

            def step(b, g):
                s = 4 * b + g
                project, _, scores, _, _ = stages(b, g)

                def one_head_keys():
                    wait_alone(k4_ready, s + 1)
                    if not early(b, g, 4):
                        wait_alone(b_unit, (s - 3) * NU)
                    for j in range(HG):
                        nc.gpsimd.tensor_scalar(kh[:, g, j, :], k4[:, g % 2, :], col(K_MASK + j), col(K_NEG + j),
                                                ALU.mult, ALU.add).then_inc(kh_ready, 1)

                def select(pair):
                    n = s - 2
                    row = pr[:, g % 2, pair, :]
                    wait_alone(exped, n * NU + 5 * (pair + 1))
                    full = row[:, 0:2048].rearrange("p (a b c) -> p a b c", a=2, b=2)[:, :, :, 0:P]
                    third = row[:, 0:2048].rearrange("p (a c) -> p a c", a=2)[:, :, 896:1024]
                    second = row[:, 2048:2560].rearrange("p (a c) -> p a c", a=2)[:, :, 0:P]
                    for d, pattern in ((full, [[0, 2], [0, 2], [1, P]]), (third, [[0, 2], [1, P]]),
                                       (second, [[0, 2], [1, P]])):
                        nc.gpsimd.affine_select(out=d, in_=d, pattern=pattern, compare_op=ALU.is_ge, fill=0.0, base=0,
                                                channel_multiplier=-1).then_inc(selected, 1)

                if scores:
                    select(0)
                if project:
                    one_head_keys()
                taken, _ = normalisations(b, g)
                if taken is not None:
                    inverse_roots(taken, normalised(taken, b))
                if scores:
                    select(1)

            blocks(pool, step)
            inverse_roots(1, B - 1)
            pool.wait_ge(blanked, 16 * PARTS)
            pool.wait_ge(prep2, 7)
            pool.wait_ge(row_copied, B)

            def places_set(h, k):
                if k:
                    pool.wait_ge(rows_out[h], 16 * NTP)
                nc.gpsimd.tensor_copy(xr[:, h * NTP:(h + 1) * NTP, D].bitcast(I32), ids[:, k, :]).then_inc(ids_set, 1)
                pool.wait_ge(ids_set, KTOP * h + k + 1)
                if not k:
                    pool.wait_ge(routed, h + 1)

            def scatter(h, k, t):
                nc.gpsimd.indirect_dma_start(x_sorted[h], bass.IndirectOffsetOnAxis(ap=pos[:, h, k, t:t + 1], axis=0),
                                             xr[:, h * NTP + t, :], None).then_inc(rows_out[h], 16)

            for k in range(KTOP):
                places_set(0, k)
                for t in range(NTP):
                    scatter(0, k, t)

            def send(jb, k, _, h):
                if isinstance(jb, int) and jb < KTOP:
                    if k == 0:
                        places_set(1, jb)
                    for t in range(k * NTP // NX, (k + 1) * NTP // NX):
                        scatter(1, jb, t)
                if isinstance(jb, int) and not 0 <= NX * jb + k - 2 < NJ:
                    return
                j, q = NX * jb + k - 2, (k - 2) % NX
                if isinstance(jb, int):
                    h = j // NJP
                wait_alone(t_y, j + 1)
                nc.gpsimd.indirect_dma_start(
                    y_token[h], bass.IndirectOffsetOnAxis(ap=xt[:, q, D:ROW].bitcast(U32), axis=0), y[:, q, :], None,
                    bounds_check=TP * KTOP - 1, oob_is_err=False).then_inc(y_out[q], 16)

            tile_blocks(pool, send)

        @block.scalar
        def _(act_e):
            def high_part_of_x(kind, batch):
                act_e.wait_ge(xt_ready[kind], batch + 1)
                nc.scalar.activation(x_hi[:, bass.ds(batch * S, S)], ps_m[1][:, :], ACT.Copy)\
                    .then_inc(xhi_ready[kind], 1)

            def rows_copied(batch):
                act_e.wait_ge(xn_ready[1], QT * (batch + 1))
                nc.scalar.activation(xr[:, bass.ds(batch * QT, QT), 0:D], xn[:, 1, :, :], ACT.Copy)\
                    .then_inc(row_copied, 1)

            high_part_of_x(0, 0)

            def step(b, g):
                s = 4 * b + g
                project, _, scores, values, output = stages(b, g)
                i0 = ((g - 2) % G) * NU

                def probs(u):
                    n = s - 2
                    act_e.wait_ge(b_unit, n * NU + u + 1)
                    if u == 0 and not early(b, g, 4):
                        act_e.wait_ge(pv_done, n - 1)
                    pair, k = divmod(u, 5)
                    nc.scalar.activation(pr[:, g % 2, pair, 512 * k:512 * (k + 1)], ps_b[SBANK[i0 + u]][:, :],
                                         ACT.Exp, scale=float(DK) ** -0.5).then_inc(exped, 1)

                def high_part(proj, low_ready, high_ready, dst, src, scale):
                    act_e.wait_ge(proj, s + 1)
                    if not early(b, g, 1):
                        act_e.wait_ge(low_ready, s)
                    nc.scalar.activation(dst[:, :], src[:, :], ACT.Copy, scale=scale).then_inc(high_ready, 1)

                def values_out():
                    act_e.wait_ge(v_proj, b + 1)
                    if not early(b, g, 4):
                        act_e.wait_ge(pv_done, s - 2)
                    else:
                        act_e.wait_ge(prep2, 3)
                    nc.scalar.activation(va.rearrange("p t g h c -> p (t g h) c")[:, :, 0:DK],
                                         ps_m[0][:, :].rearrange("p (a d) -> p a d", d=DK),
                                         ACT.Copy, scale=1.0 / (XS * WS)).then_inc(v_ready, 1)

                def outputs_out():
                    n = s - 3
                    act_e.wait_ge(pv_done, n + 1)
                    if not early(b, g, 4):
                        act_e.wait_ge(o_t, n)
                    nc.scalar.activation(ot[:, :], ps_o[:, :], ACT.Copy).then_inc(o_out, 1)

                _, turned = normalisations(b, g)
                for what, u in ACT_ORDER:
                    if what == "e" and scores:
                        probs(u)
                    elif what == "q" and project:
                        high_part(q_proj, q4_ready, qhi_ready, hi_q, ps_m[0], col(K_SQ))
                    elif what == "k" and project:
                        high_part(k_proj, k4_ready, khi_ready, hi_k, ps_m[1], col(K_SK))
                    elif what == "v" and project and g == G - 2:
                        values_out()
                    elif what == "t" and output:
                        act_e.wait_ge(at_t, b)
                        nc.scalar.activation(attn_t[:, :], ps_m[0][:, :], ACT.Copy).then_inc(at_out, 1)
                    elif what == "o" and values:
                        outputs_out()
                    elif what == "h" and turned is not None:
                        high_part_of_x(turned, normalised(turned, b))
                    elif what == "c" and turned == 1:
                        rows_copied(normalised(turned, b))
                if early(b, g, 8) and s >= 3 and s < 7:
                    act_e.wait_ge(wf_in, 48)
                    cols = slice((s - 3) * NE * F // 4, (s - 2) * NE * F // 4)
                    nc.scalar.activation(wu_hi[:, cols], wu_raw[:, cols], ACT.Copy, scale=US).then_inc(wu_high, 1)

            blocks(act_e, step)
            high_part_of_x(1, B - 1)
            rows_copied(B - 1)
            act_e.wait_ge(logits_ready, 1)
            nc.scalar.activation(sig[:, :, :], lg[:, :, :], ACT.Exp, scale=-1.0).then_inc(exp_ready, 1)
            act_e.wait_ge(wf_in, 48)

            def shared_act(b, par):
                for f in range(FC):
                    act_e.wait_ge(sh_up, FC * b + f + 1)
                    if not early(b, 0, 2 * G):
                        act_e.wait_ge(sh_down, b - 1)
                    nc.scalar.activation(act[:, par, f, :], sh_bank[f][:, :], ACT.Gelu, bias=sbu[:, f:f + 1],
                                         scale=1.0 / (XS * US)).then_inc(sh_act, 1)

            shared_act(0, 0)
            shared_act(1, 1)
            with act_e.Fori(1, B // 2) as m:
                shared_act(2 * m, 0)
                shared_act(2 * m + 1, 1)

            def tile_act(jb, k, e, h):
                j = NX * jb + k
                first = isinstance(jb, int) and jb == 0
                if not isinstance(jb, int) or j < NJ:
                    act_e.wait_ge(t_turned, j + 1)
                    if not (first and k < 2):
                        act_e.wait_ge(t_up, j - 1)
                    nc.scalar.activation(xh[:, k % 2, :], ps_m[k % 2][:, 0:P], ACT.Copy).then_inc(t_hi, 1)
                if not isinstance(jb, int) or 0 <= j - 1 < NJ:
                    act_e.wait_ge(t_up, j)
                    if not (first and k < 3):
                        act_e.wait_ge(t_down, j - 2)
                    q = (k - 1) % 2
                    for f in range(FC):
                        ins = nc.scalar.activation(act2[:, q, f, :], ps_a[q][:, f * P:(f + 1) * P], ACT.Gelu,
                                                   bias=bu[:, bass.ds(e[k] * FC + f, 1)], scale=1.0 / (XS * US))
                    ins.then_inc(t_act, 1)

            act_e.wait_ge(tables_ready, 2 + 2 * PARTS)
            act_e.wait_ge(bias_in, 32)
            tile_blocks(act_e, tile_act, lambda jb: numbers(te_up, jb, mybir.EngineType.Activation))

        @block.vector
        def _(dve):
            v = nc.vector

            def statistics(kind, batch):
                for i in range(QT):
                    t = batch * QT + i
                    v.bn_stats(stats[:, kind, i, :], x[:, bass.ds(t, 1), :]).then_inc(bn_ready[kind], 1)
                dve.wait_ge(bn_ready[kind], QT * (batch + 1))
                dve.sem_inc(dve_passed, 1)
                for i in range(QT):
                    v.bn_aggr(mv[:, kind, i, :], stats[:, kind, i, :]).then_inc(mv_ready[kind], 1)

            def normalise(kind, batch):
                dve.wait_ge(rstd_ready[kind], batch + 1)
                for i in range(QT):
                    t = batch * QT + i
                    v.tensor_scalar(xn[:, kind, i, :], x[:, bass.ds(t, 1), :], mv[:, kind, i, 0:1], rstd[:, kind, i:i + 1],
                                    ALU.subtract, ALU.mult).then_inc(xn_ready[kind], 1)

            def low_part_of_x(kind, batch):
                dve.wait_ge(xhi_ready[kind], batch + 1)
                cols = bass.ds(batch * S, S)
                v.tensor_tensor(x_lo[:, cols], ps_m[1][:, :], x_hi[:, cols], ALU.subtract)\
                    .then_inc(xlo_ready[kind], 1)

            def weights_prepared():
                dve.wait_ge(wqkv_in, 16)
                v.tensor_scalar(w_hi[:, :], wqkv[:, :], WS, None, ALU.mult).then_inc(prep, 1)
                dve.wait_ge(prep, 1)
                v.scalar_tensor_tensor(w_lo[:, :], wqkv[:, :], WS, w_hi[:, :], ALU.mult, ALU.subtract)\
                    .then_inc(prep, 1)

            def biases_split():
                dve.wait_ge(bias_in, 32)
                rest = bd[:, E * D:]
                for r in range(3):
                    v.tensor_copy(bpart[:, r, :], rest).then_inc(bias_split, 1)
                    dve.wait_ge(bias_split, 3 * r + 1)
                    if r == 0:
                        v.tensor_scalar(bd_rows[:, :], bpart[:, r, :], col(K_ROW), None, ALU.mult)\
                            .then_inc(bias_split, 1)
                    else:
                        v.scalar_tensor_tensor(bd_rows[:, :], bpart[:, r, :], col(K_ROW + r), bd_rows[:, :],
                                               ALU.mult, ALU.add).then_inc(bias_split, 1)
                    if r < 2:
                        v.tensor_tensor(brest[:, r, :], rest, bpart[:, r, :], ALU.subtract).then_inc(bias_split, 1)
                        dve.wait_ge(bias_split, 3 * r + 3)
                        rest = brest[:, r, :]

            dve.wait_ge(x_in, 16)
            statistics(0, 0)
            weights_prepared()
            normalise(0, 0)
            dve.wait_ge(prep, 2)
            for r in range(3):
                v.tensor_copy(rep_hi[:, :, :, r, :], w_hi[:, 0:2 * D].rearrange("p (a h d) -> p a h d", a=2, h=H))\
                    .then_inc(prep, 1)
            low_part_of_x(0, 0)
            for r in range(3):
                v.tensor_copy(rep_lo[:, :, :, r, :], w_lo[:, 0:2 * D].rearrange("p (a h d) -> p a h d", a=2, h=H))\
                    .then_inc(prep, 1)
            dve.wait_ge(const_in, 16)
            for dst, src in ((identb, C_ID), (causal, C_CAUSAL)):
                v.tensor_copy(dst[:, :], const[:, src:src + P]).then_inc(prep, 1)
            assert PREP == 10

            def last_weights():
                dve.wait_ge(w_in, 48)
                v.tensor_scalar(gw_hi[:, :], gw[:, :], GS, None, ALU.mult).then_inc(ffn_prep, 1)
                for dst, src in ((onesb, C_ONES), (beforeb, C_BEFORE)):
                    v.tensor_copy(dst[:, :], const[:, src:src + P]).then_inc(ffn_prep, 1)
                dve.wait_ge(ffn_prep, 1)
                v.scalar_tensor_tensor(gw_lo[:, :], gw[:, :], GS, gw_hi[:, :], ALU.mult, ALU.subtract)\
                    .then_inc(ffn_prep, 1)
                biases_split()

            def low_up_weights(piece):
                dve.wait_ge(wu_high, piece + 1)
                cols = slice(piece * NE * F // 4, (piece + 1) * NE * F // 4)
                v.scalar_tensor_tensor(wu_lo[:, cols], wu_raw[:, cols], US, wu_hi[:, cols], ALU.mult, ALU.subtract)\
                    .then_inc(wu_low, 1)

            def add_residual(b):
                dve.wait_ge(wo_done, b)
                xb = x[:, bass.ds((b - 1) * QT, QT), :].rearrange("p t d -> p (t d)")
                v.tensor_tensor(xb, ps_m[1][:, :], xb, ALU.add).then_inc(x2_ready, 1)

            def step(b, g):
                s = 4 * b + g
                project, maxima, scores, values, output = stages(b, g)
                first = isinstance(b, int) and b == 0

                def low_part_of_q():
                    dve.wait_ge(qhi_ready, s + 1)
                    if not (first and g < 2):
                        dve.wait_ge(qf_ready, s - 1)
                    v.scalar_tensor_tensor(q4[:, g % 2, :], ps_m[0][:, :], 1.0 / (XS * WS), hi_q[:, :], ALU.mult,
                                           ALU.subtract).then_inc(q4_ready, 1)

                def low_part_of_k():
                    dve.wait_ge(khi_ready, s + 1)
                    if not (first and g < 2):
                        dve.wait_ge(kh_ready, HG * (s - 1))
                    v.scalar_tensor_tensor(k4[:, g % 2, :], ps_m[1][:, :], 1.0 / (XS * WS), hi_k[:, :], ALU.mult,
                                           ALU.subtract).then_inc(k4_ready, 1)

                def maximum(u):
                    n, par = s - 1, (g - 1) % 2
                    dve.wait_ge(a_unit, n * NU + u + 1)
                    if u == 0 and not (first and g < 3):
                        dve.wait_ge(m_t, n - 1)
                    elif u == 0:
                        dve.wait_ge(prep2, 1)
                    src = ps_a[u % 2]
                    h, t, _ = UNITS[u][0]
                    at = 32 * h + 3 * DK
                    if REDS[u] == 1 and len(UNITS[u]) == 2:
                        v.tensor_reduce(mt[:, par, QT - 1 - t, at:at + 33:32],
                                        src[:, :].rearrange("p (a c) -> p a c", a=2), AX, ALU.max).then_inc(maxed, 1)
                        return
                    for h, t, c in UNITS[u]:
                        v.tensor_reduce(mt[:, par, QT - 1 - t, at:at + 1], src[:, c:c + WIDE[t]], AX, ALU.max)\
                            .then_inc(maxed, 1)

                def queries_with_maxima():
                    n, par = s - 2, g % 2
                    dve.wait_ge(m_t, n + 1)
                    dve.wait_ge(q4_ready, n + 1)
                    if not first:
                        dve.wait_ge(b_unit, NU * (n - 1))
                    v.tensor_tensor(qf[:, par, :], q4[:, par, :], ps_m[1][:, :], ALU.add).then_inc(qf_ready, 1)

                def normalise_outputs():
                    n, gi = s - 3, (g - 3) % G
                    dve.wait_ge(o_t, n + 1)
                    o = ps_m[0][:, :].rearrange("p (t h c) -> p t h c", t=QT, h=HG)
                    if not first:
                        dve.wait_ge(normed, n)
                    v.reciprocal(rec[:, :, :], o[:, :, :, DK]).then_inc(rec_ready, 1)
                    dve.wait_ge(rec_ready, n + 1)
                    out = attn[:, :, gi * 32:gi * 32 + 32].rearrange("p t (h d) -> p t h d", h=HG)
                    v.tensor_tensor(out, o[:, :, :, 0:DK],
                                    rec[:, :, :].unsqueeze(3).to_broadcast([P, QT, HG, DK]), ALU.mult)\
                        .then_inc(normed, 1)

                taken, turned = normalisations(b, g)
                for what, u in DVE_ORDER:
                    if what == "r" and maxima:
                        maximum(u)
                    elif what == "f" and scores:
                        queries_with_maxima()
                    elif what == "q" and project:
                        low_part_of_q()
                    elif what == "k" and project:
                        low_part_of_k()
                    elif what == "x" and output:
                        add_residual(b)
                    elif what == "n" and values:
                        normalise_outputs()
                    elif what == "s" and taken is not None:
                        if taken == 1:
                            dve.wait_ge(x2_ready, b)
                        elif early(b, g, 2):
                            dve.wait_ge(x_in2, 16)
                        statistics(taken, normalised(taken, b))
                    elif what == "y" and turned is not None:
                        normalise(turned, normalised(turned, b))
                    elif what == "l" and turned is not None:
                        low_part_of_x(turned, normalised(turned, b))
                if early(b, g, 3) and s == 2:
                    last_weights()
                if early(b, g, 8) and s >= 4:
                    low_up_weights(s - 4)
                if first and g == G - 1:
                    dve.sem_inc(x2_ready, 1)

            blocks(dve, step)
            dve.wait_ge(x2_ready, B + 1)
            statistics(1, B - 1)
            normalise(1, B - 1)
            low_part_of_x(1, B - 1)
            count = [0]

            def then(ins):
                ins.then_inc(topk, 1)
                count[0] += 1
                dve.wait_ge(topk, count[0])

            dve.wait_ge(gate_done, 1)
            v.scalar_tensor_tensor(lg[:, :, :], ps_m[0][:, 0:NT * E].rearrange("p (t e) -> p t e", e=E),
                                   1.0 / (XS * GS), gb[:, :].unsqueeze(1).to_broadcast([P, NT, E]), ALU.mult, ALU.add)\
                .then_inc(logits_ready, 1)
            dve.wait_ge(exp_ready, 1)
            then(v.tensor_scalar(sig[:, :, :], sig[:, :, :], 1.0, None, ALU.add))
            then(v.reciprocal(sig[:, :, :], sig[:, :, :]))

            def per_expert(ap):
                return ap.unsqueeze(1).to_broadcast([P, NTP, E])

            def per_token(ap, n=E):
                return ap.unsqueeze(2).to_broadcast([P, NTP, n])

            def two_best(h):
                ts = slice(h * NTP, (h + 1) * NTP)
                left = sig[:, ts, :]
                for r in range(KTOP):
                    if r:
                        then(v.scalar_tensor_tensor(rest_of[:, :, :], oh[:, h, 0, :, :], -2.0, left, ALU.mult, ALU.add))
                        left = rest_of[:, :, :]
                    then(v.tensor_reduce(score[:, r, ts], left, AX, ALU.max))
                    then(v.tensor_tensor(tied[:, :, :], left, per_token(score[:, r, ts]), ALU.is_equal))
                    then(v.tensor_tensor(tied[:, :, :], tied[:, :, :], per_expert(col(K_REV, E)), ALU.mult))
                    then(v.tensor_reduce(key[:, r, ts], tied[:, :, :], AX, ALU.max))
                    then(v.tensor_tensor(oh[:, h, r, :, :], per_expert(col(K_REV, E)), per_token(key[:, r, ts]),
                                         ALU.is_equal))
                v.tensor_tensor(chosen[:, ts, :], oh[:, h, 0, :, :], oh[:, h, 1, :, :], ALU.add)\
                    .then_inc(chosen_ready, 1)

            def two_weights(h):
                ts = slice(h * NTP, (h + 1) * NTP)
                then(v.tensor_tensor(den[:, ts], score[:, 0, ts], score[:, 1, ts], ALU.add))
                then(v.tensor_scalar(den[:, ts], den[:, ts], 1e-6, None, ALU.add))
                then(v.reciprocal(den[:, ts], den[:, ts]))
                then(v.tensor_tensor(wgt[:, :, ts], score[:, :, ts],
                                     den[:, ts].unsqueeze(1).to_broadcast([P, KTOP, NTP]), ALU.mult))

            def places(h):
                dve.wait_ge(ranked, h + 1)
                at = 2 * NTP * E * h
                rank = ps_m[1][:, at:at + NTP * E].rearrange("p (t e) -> p t e", e=E)
                total = ps_m[1][:, at + NTP * E:at + NTP * E + E]
                then(v.scalar_tensor_tensor(over[:, :, :], total.unsqueeze(2).to_broadcast([P, E, NTP]), 1.0 / P,
                                            col(K_TILE, NTP).unsqueeze(1).to_broadcast([P, E, NTP]), ALU.mult,
                                            ALU.is_gt))
                then(v.tensor_reduce(tiles[:, :], over[:, :, :], AX, ALU.add))
                then(v.tensor_tensor(share[:, :, :, :].rearrange("p a e f -> p (a e) f"),
                                     tiles[:, :].unsqueeze(1).to_broadcast([P, 2 * E, E]),
                                     col(K_ENDS, 2 * E * E).rearrange("p (a f) -> p a f", f=E), ALU.mult))
                then(v.tensor_reduce(ends[:, :, :], share[:, :, :, :], AX, ALU.add))
                then(v.tensor_tensor(place[:, :, :], rank, per_expert(ends[:, 1, :]), ALU.add))
                for r in range(KTOP):
                    ins = v.tensor_tensor(ohs[:, r, :, :], oh[:, h, r, :, :], place[:, :, :], ALU.mult)
                then(ins)
                then(v.tensor_reduce(posf[:, h, :, :], ohs[:, :, :, :], AX, ALU.add))
                v.tensor_copy(pos[:, h, :, :], posf[:, h, :, :]).then_inc(routed, 1)
                then(v.tensor_tensor(past[:, :, :], col(K_TILE, NJP).unsqueeze(2).to_broadcast([P, NJP, E]),
                                     ends[:, 0, :].unsqueeze(1).to_broadcast([P, NJP, E]), ALU.is_ge))
                then(v.tensor_reduce(te[:, :], past[:, :, :], AX, ALU.add))
                for lag, table in ((1, te_up), (2, te_down)):
                    v.tensor_scalar(table[:, h * NJP + lag:(h + 1) * NJP + lag], te[:, :], float(E - 1), None,
                                    ALU.min).then_inc(tables_ready, 1)

            def shared_added(b, par):
                dve.wait_ge(sh_down, b + 1)
                xb = x[:, bass.ds(b * QT, QT), :].rearrange("p t d -> p (t d)")
                v.scalar_tensor_tensor(xb, ps_down[par][:, :], 0.1, xb, ALU.mult, ALU.add).then_inc(sh_added, 1)

            for table in (te_up, te_down):
                v.memset(table[:, :], 0).then_inc(tables_ready, 1)
            dve.wait_ge(tables_ready, 2)
            two_best(0)
            two_weights(0)
            places(0)
            shared_added(0, 0)
            two_best(1)
            two_weights(1)
            shared_added(1, 1)
            places(1)
            with dve.Fori(1, B // 2) as m:
                shared_added(2 * m, 0)
                shared_added(2 * m + 1, 1)

            def add_experts(t, i, q):
                xq = x[:, bass.ds(t, 1), :].rearrange("p a d -> p (a d)")
                for r in range(KTOP):
                    if r:
                        dve.wait_ge(summed0, t + 1)
                    v.scalar_tensor_tensor(xq, yb[:, i, q, r, :], wgt[:, r, bass.ds(t, 1)], xq, ALU.mult, ALU.add)\
                        .then_inc(summed if r else summed0, 1)

            def tile_parts(jb, k, e, h):
                j = NX * jb + k
                first = isinstance(jb, int) and jb == 0
                if not isinstance(jb, int) or j < NJ:
                    dve.wait_ge(t_hi, j + 1)
                    if not (first and k < 2):
                        dve.wait_ge(t_up, j - 1)
                    v.tensor_tensor(xl[:, k % 2, :], ps_m[k % 2][:, 0:P], xh[:, k % 2, :], ALU.subtract)\
                        .then_inc(t_lo, 1)
                if not isinstance(jb, int) or 0 <= j - 2 < NJ:
                    dve.wait_ge(t_down, j - 1)
                    q = (k - 2) % NX
                    sent = jb if k >= 2 else jb - 1
                    if not isinstance(jb, int) or sent > 0:
                        dve.wait_ge(y_out[q], 16 * sent)
                    v.tensor_tensor(y[:, q, :], ps_down[k % 2][:, 0:D], bd[:, bass.ds(e[k] * D, D)], ALU.add)\
                        .then_inc(t_y, 1)

                if isinstance(jb, int) and jb == NJBP and k == 0:
                    dve.sem_inc(summed, QT)
                elif not isinstance(jb, int) and h == 1 and COMBINE <= k < COMBINE + QT:
                    if k == COMBINE:
                        dve.wait_ge(yb_in, 16 * QT * (jb - NJBP))
                    add_experts((jb - (NJBP + 1)) * QT + k - COMBINE, 0, k - COMBINE)

            dve.wait_ge(tables_ready, 2 + 2 * PARTS)
            tile_blocks(dve, tile_parts, lambda jb: numbers(te_down, jb, mybir.EngineType.DVE))
            for i in range(BP):
                dve.wait_ge(yb_in_last[i], 16 * QT)
                for q in range(QT):
                    add_experts((BP + i) * QT + q, i, q)

        @block.tensor
        def _(pe):
            mm = nc.tensor.matmul

            def turned(kind, batch):
                pe.wait_ge(xn_ready[kind], QT * (batch + 1))
                for i in range(QT):
                    last = nc.tensor.transpose(ps_m[1][:, i * P:(i + 1) * P], xn[:, kind, i, :], ident)
                last.then_inc(xt_ready[kind], 1)

            pe.wait_ge(const_in, 16)
            turned(0, 0)
            pe.wait_ge(prep, PREP)
            pe.wait_ge(rep_zeroed, 2)

            def project_into(dst, a, b, g):
                xs = bass.ds(b * S, S)
                hi = rep_hi[:, a, g * HG:(g + 1) * HG, :, :].rearrange("p h r d -> p (h r d)")
                lo = rep_lo[:, a, g * HG:(g + 1) * HG, :, :].rearrange("p h r d -> p (h r d)")
                mm(dst[:, :], hi, x_hi[:, xs], start=True, stop=False)
                mm(dst[:, :], hi, x_lo[:, xs], start=False, stop=False)
                return mm(dst[:, :], lo, x_hi[:, xs], start=False, stop=True)

            def project_q(b, g, s):
                if g == 0:
                    pe.wait_ge(xlo_ready[0], b + 1)
                if not early(b, g, 4):
                    pe.wait_ge(normed, s - 3)
                elif g == G - 1:
                    pe.wait_ge(v_ready, 1)
                elif g:
                    pe.wait_ge(q4_ready, s)
                project_into(ps_m[0], 0, b, g).then_inc(q_proj, 1)

            def project_k(b, g, s):
                if not early(b, g, 2):
                    pe.wait_ge(qf_ready, s - 1)
                elif g:
                    pe.wait_ge(k4_ready, s)
                project_into(ps_m[1], 1, b, g).then_inc(k_proj, 1)

            def project_v(b, s):
                pe.wait_ge(q4_ready, s + 1)
                for i in range(QT):
                    xs = bass.ds(b * S + i * P, P)
                    dst = ps_m[0][:, i * P:(i + 1) * P]
                    mm(dst, x_hi[:, xs], w_hi[:, 2 * D:3 * D], start=True, stop=False)
                    mm(dst, x_hi[:, xs], w_lo[:, 2 * D:3 * D], start=False, stop=False)
                    last = mm(dst, x_lo[:, xs], w_hi[:, 2 * D:3 * D], start=False, stop=True)
                last.then_inc(v_proj, 1)

            def step(b, g):
                s = 4 * b + g
                project, maxima, scores, values, output = stages(b, g)
                def a_scores(u):
                    n, gi, par = s - 1, (g - 1) % G, (g - 1) % 2
                    if u == 0:
                        pe.wait_ge(q4_ready, n + 1)
                        pe.wait_ge(kh_ready, HG * (n + 1))
                    if u >= 2:
                        pe.wait_ge(maxed, NRED * n + RED_TO[u - 2])
                    elif not early(b, g, 2):
                        pe.wait_ge(maxed, NRED * (n - 1) + RED_TO[u + NU - 2])
                    dst = ps_a[u % 2]
                    for h, t, c in UNITS[u]:
                        i = QT - 1 - t
                        w = WIDE[t]
                        mm(dst[:, c:c + w], q4[:, par, i * P:(i + 1) * P], kh[:, gi, h, 0:w], start=True, stop=False)
                        last = mm(dst[:, c + w - P:c + w], identb[:, :], causal[:, :], start=False, stop=True)
                    last.then_inc(a_unit, 1)

                def b_scores(u):
                    n, gi, par = s - 2, (g - 2) % G, g % 2
                    if u == 0:
                        pe.wait_ge(qf_ready, n + 1)
                    i0 = gi * NU + u
                    prev = before(i0)
                    if prev >= 0 or not early(b, g, 4):
                        pe.wait_ge(exped, NU * (n - gi) + prev + 1)
                    dst = ps_b[SBANK[i0]]
                    for h, t, c in UNITS[u]:
                        last = mm(dst[:, c:c + WIDE[t]], kh[:, gi, h, t * P:(t + 1) * P], qf[:, par, t * P:S],
                                  start=True, stop=True)
                    last.then_inc(b_unit, 1)

                def weighted_values(t):
                    n, gi, par = s - 3, (g - 3) % G, (g - 3) % 2
                    if t == 0:
                        pe.wait_ge(exped, NU * (n + 1))
                        pe.wait_ge(selected, 6 * (n + 1))
                        pe.wait_ge(v_ready, b + 1 if g == G - 1 else b)
                        if not early(b, g, 4):
                            pe.wait_ge(o_out, n)
                    for h in range(HG):
                        at = PROB_AT[(h % 2, t)]
                        last = mm(ps_o[32 * h:32 * h + 32, t * P:S], va[:, t, gi, h, :],
                                  pr[:, par, h // 2, at:at + WIDE[t]], start=(t == 0), stop=(t == QT - 1))
                    if t == QT - 1:
                        last.then_inc(pv_done, 1)

                def outputs_turned():
                    n = s - 3
                    pe.wait_ge(o_out, n + 1)
                    if output:
                        pe.wait_ge(at_out, b)
                    elif project and g == G - 2:
                        pe.wait_ge(v_ready, b + 1)
                    elif project:
                        pe.wait_ge(q4_ready, s + 1)
                    else:
                        pe.wait_ge(normed, n)
                    for i in range(QT):
                        last = nc.tensor.transpose(ps_m[0][:, i * P:(i + 1) * P], ot[:, i * P:(i + 1) * P], ident)
                    last.then_inc(o_t, 1)

                def attention_turned():
                    pe.wait_ge(normed, 4 * b)
                    if project:
                        pe.wait_ge(q4_ready, s + 1)
                    for i in range(QT):
                        last = nc.tensor.transpose(ps_m[0][:, i * P:(i + 1) * P], attn[:, i, :], ident)
                    last.then_inc(at_t, 1)

                def output_projected():
                    pe.wait_ge(at_out, b)
                    if project:
                        pe.wait_ge(k4_ready, s + 1)
                    else:
                        pe.wait_ge(xlo_ready[1], b - 1)
                    for i in range(QT):
                        last = mm(ps_m[1][:, i * P:(i + 1) * P], attn_t[:, i * P:(i + 1) * P], wo[:, :], start=True,
                                  stop=True)
                    last.then_inc(wo_done, 1)

                def maxima_turned():
                    n, par = s - 2, g % 2
                    pe.wait_ge(maxed, NRED * (n + 1))
                    _, before_turned = normalisations(b, g - 1)
                    if g == 0:
                        pe.wait_ge(x2_ready, b)
                    elif before_turned is not None:
                        pe.wait_ge(xlo_ready[before_turned], normalised(before_turned, b) + 1)
                    elif project:
                        pe.wait_ge(k4_ready, s)
                    else:
                        pe.wait_ge(qf_ready, n)
                    for i in range(QT):
                        last = nc.tensor.transpose(ps_m[1][:, i * P:(i + 1) * P], mt[:, par, i, :], ident)
                    last.then_inc(m_t, 1)

                _, to_turn = normalisations(b, g)
                for what, u in PE_ORDER:
                    if what == "a" and maxima:
                        a_scores(u)
                    elif what == "b" and scores:
                        b_scores(u)
                    elif what == "q" and project:
                        project_q(b, g, s)
                    elif what == "k" and project:
                        project_k(b, g, s)
                    elif what == "v" and project and g == G - 2:
                        project_v(b, s)
                    elif what == "w" and values:
                        weighted_values(u)
                    elif what == "o" and values:
                        outputs_turned()
                    elif what == "t" and output:
                        attention_turned()
                    elif what == "j" and output:
                        output_projected()
                    elif what == "m" and scores:
                        maxima_turned()
                    elif what == "x" and to_turn is not None:
                        if project:
                            pe.wait_ge(k4_ready, s + 1)
                        else:
                            pe.wait_ge(qf_ready, B * G)
                        turned(to_turn, normalised(to_turn, b))

            blocks(pe, step)
            def gate(tiles):
                for t in tiles:
                    xs = slice(t * P, (t + 1) * P)
                    dst = ps_m[0][:, t * E:(t + 1) * E]
                    mm(dst, x_hi[:, xs], gw_hi[:, :], start=True, stop=False)
                    mm(dst, x_hi[:, xs], gw_lo[:, :], start=False, stop=False)
                    last = mm(dst, x_lo[:, xs], gw_hi[:, :], start=False, stop=True)
                return last

            def ranks(h):
                pe.wait_ge(chosen_ready, h + 1)
                at = 2 * NTP * E * h
                ch = chosen[:, h * NTP:(h + 1) * NTP, :].rearrange("p t e -> p (t e)")
                mm(ps_m[1][:, at:at + NTP * E], beforeb[:, :], ch, start=True, stop=False)
                for back in range(1, NTP):
                    n = (NTP - back) * E
                    mm(ps_m[1][:, at + back * E:at + NTP * E], allb[:, :], ch[:, 0:n], start=False,
                       stop=(back == NTP - 1))
                for t in range(NTP):
                    last = mm(ps_m[1][:, at + NTP * E:at + NTP * E + E], allb[:, :], ch[:, t * E:(t + 1) * E],
                              start=(t == 0), stop=(t == NTP - 1))
                last.then_inc(ranked, 1)

            def shared_up(b):
                xs = bass.ds(b * S, S)
                for f in range(FC):
                    if not early(b, 0, G):
                        pe.wait_ge(sh_act, FC * (b - 1) + f + 1)
                    ws = slice(E * F + f * P, E * F + (f + 1) * P)
                    mm(sh_bank[f][:, :], wu_hi[:, ws], x_hi[:, xs], start=True, stop=False)
                    mm(sh_bank[f][:, :], wu_hi[:, ws], x_lo[:, xs], start=False, stop=False)
                    mm(sh_bank[f][:, :], wu_lo[:, ws], x_hi[:, xs], start=False, stop=True).then_inc(sh_up, 1)

            def shared_down(b, par):
                pe.wait_ge(sh_act, FC * (b + 1))
                if not early(b, 0, 2 * G):
                    pe.wait_ge(sh_added, b - 1)
                for i in range(QT):
                    dst = ps_down[par][:, i * P:(i + 1) * P]
                    for f in range(FC):
                        ws = slice((E * FC + f) * D, (E * FC + f + 1) * D)
                        mm(dst, act[:, par, f, i * P:(i + 1) * P], wd[:, ws], start=(f == 0), stop=False)
                    last = mm(dst, onesb[:, :], bd_rows[:, :], start=False, stop=True)
                last.then_inc(sh_down, 1)

            pe.wait_ge(ffn_prep, 4)
            pe.wait_ge(normed, B * G)
            gate(range(NT - QT))
            pe.wait_ge(x2_ready, B + 1)
            turned(1, B - 1)
            pe.wait_ge(xlo_ready[1], B)
            gate(range(NT - QT, NT)).then_inc(gate_done, 1)
            pe.wait_ge(wu_low, 4)
            pe.wait_ge(bias_split, 8)
            pe.wait_ge(prep2, 7)
            shared_up(0)
            ranks(0)
            shared_up(1)
            shared_down(0, 0)
            shared_up(2)
            shared_down(1, 1)
            ranks(1)
            with pe.Fori(1, B // 2 - 1) as m:
                shared_up(2 * m + 1)
                shared_down(2 * m, 0)
                shared_up(2 * m + 2)
                shared_down(2 * m + 1, 1)
            shared_up(B - 1)
            shared_down(B - 2, 0)
            shared_down(B - 1, 1)
            pe.wait_ge(sh_added, B)
            pe.wait_ge(tables_ready, 2 + 2 * PARTS)

            def experts(jb):
                return numbers(te_up, jb, mybir.EngineType.PE), numbers(te_down, jb, mybir.EngineType.PE)

            def tile_mms(jb, k, e, h):
                j = NX * jb + k
                first = isinstance(jb, int) and jb == 0
                if not isinstance(jb, int) or j < NJ:
                    pe.wait_ge(xt_in[k], 16 * (jb + 1))
                    nc.tensor.transpose(ps_m[k % 2][:, 0:P], xt[:, k, 0:D], ident).then_inc(t_turned, 1)
                if not isinstance(jb, int) or 0 <= j - 1 < NJ:
                    q = (k - 1) % 2
                    pe.wait_ge(t_lo, j)
                    for f in range(FC):
                        dst = ps_a[q][:, f * P:(f + 1) * P]
                        ws = bass.ds(e[0][k] * F + f * P, P)
                        mm(dst, wu_hi[:, ws], xh[:, q, :], start=True, stop=False)
                        mm(dst, wu_hi[:, ws], xl[:, q, :], start=False, stop=False)
                        last = mm(dst, wu_lo[:, ws], xh[:, q, :], start=False, stop=True)
                    last.then_inc(t_up, 1)
                if not isinstance(jb, int) or 0 <= j - 2 < NJ:
                    q = k % 2
                    pe.wait_ge(t_act, j - 1)
                    if not (first and k < 4):
                        pe.wait_ge(t_y, j - 3)
                    for f in range(FC):
                        last = mm(ps_down[q][:, 0:D], act2[:, q, f, :], wd[:, bass.ds(e[1][k] * (FC * D) + f * D, D)],
                                  start=(f == 0), stop=(f == FC - 1))
                    last.then_inc(t_down, 1)

            tile_blocks(pe, tile_mms, experts)


def kernel(L0_attn_x, L0_attn_w_qkv, L0_attn_w_o, L0_ffn_gate_w, L0_ffn_gate_bias, L0_ffn_Wu, L0_ffn_bu, L0_ffn_Wd,
           L0_ffn_bd, L0_ffn_sWu, L0_ffn_sbu, L0_ffn_sWd, L0_ffn_sbd):
    import numpy as np
    import concourse.bacc as bacc
    from concourse.bass_utils import run_bass_kernel_spmd

    a = {k: np.asarray(v) for k, v in locals().items() if k.startswith("L0_")}
    c = np.ascontiguousarray
    arrays = {
        "x": c(a["L0_attn_x"].reshape(T, D)),
        "wqkv": c(a["L0_attn_w_qkv"].reshape(3 * D, D).T),
        "wo": c(a["L0_attn_w_o"].T),
        "gate": c(a["L0_ffn_gate_w"].T),
        "gbias": c(a["L0_ffn_gate_bias"]),
        "wu": c(np.concatenate([a["L0_ffn_Wu"].reshape(E * F, D), a["L0_ffn_sWu"]]).T),
        "bu": c(a["L0_ffn_bu"].reshape(E, FC, P).transpose(2, 0, 1).reshape(P, E * FC)),
        "sbu": c(a["L0_ffn_sbu"].reshape(FC, P).T),
        "wd": c(np.concatenate([a["L0_ffn_Wd"], a["L0_ffn_sWd"][None]]).reshape(E + 1, D, FC, P)
                .transpose(3, 0, 2, 1).reshape(P, (E + 1) * FC * D)),
        "bd": c(np.concatenate([a["L0_ffn_bd"], a["L0_ffn_sbd"][None]]).reshape((E + 1) * D)),
        "const": constants(),
    }
    nc = bacc.Bacc("TRN2", target_bir_lowering=False, num_devices=1)
    aps = [nc.dram_tensor(f"in_{k}", v.shape, FP32, kind="ExternalInput").ap() for k, v in arrays.items()]
    out = nc.dram_tensor("out", (T, D), FP32, kind="ExternalOutput").ap()
    program(nc, *aps, out)
    r = run_bass_kernel_spmd(nc, [{f"in_{k}": v for k, v in arrays.items()}], core_ids=[0])
    return r.results[0]["out"].reshape(B, S, D)
```

```python
import concourse.bass as bass
from concourse import mybir
from contextlib import ExitStack

FP32 = mybir.dt.float32
FP16 = mybir.dt.float16
BF16 = mybir.dt.bfloat16
U32 = mybir.dt.uint32
I32 = mybir.dt.int32
ALU = mybir.AluOpType
ACT = mybir.ActivationFunctionType
AX = mybir.AxisListType.X

P = 128
B, S, D = 8, 512, 128
H, DK = 16, 8
E, F = 8, 512
T = B * S
NT = T // P
QT = S // P
G, HG = 4, 4
FC = F // P
XS, WS, US, GS = 64.0, 64.0, 256.0, 4096.0
EPS = 1e-5
KTOP = 2
PARTS = 2
TP, NTP = T // PARTS, NT // PARTS
NX = 8
NJBP = -(-((TP * KTOP + E * (P - 1)) // P) // NX)
NJP, NJB = NJBP * NX, PARTS * NJBP
NJ = NJB * NX
BP = B // PARTS
assert BP < NJBP
COMBINE = 4
ROW = D + 1
NOWHERE = float(2 ** 30)

C_ID, C_CAUSAL, C_ONES, C_BEFORE, C_COL = 0, P, 2 * P, 3 * P, 4 * P
K_MASK, K_NEG, K_REV = 0, HG, 2 * HG
K_POW = K_REV + E
K_TILE = K_POW + QT
K_ENDS = K_TILE + NJP
K_ROW = K_ENDS + 2 * E * E
C_WIDTH = C_COL + K_ROW + 3


def constants():
    import numpy as np
    c = np.zeros((P, C_WIDTH), np.float32)
    p = np.arange(P)
    c[:, C_ID:C_ID + P] = np.eye(P)
    c[:, C_CAUSAL:C_CAUSAL + P] = np.where(p[:, None] >= p[None, :], 0.0, -1e30)
    c[0:3, C_ONES:C_ONES + P] = 1.0
    k = c[:, C_COL:]
    for j in range(HG):
        k[:, K_MASK + j] = (p // 32 == j)
        k[:, K_NEG + j] = -1.0 * (p == 32 * j + 3 * DK)
    c[:, C_BEFORE:C_BEFORE + P] = p[:, None] < p[None, :]
    k[:, K_REV:K_REV + E] = E - np.arange(E)
    k[:, K_POW:K_POW + QT] = -0.5
    k[:, K_TILE:K_TILE + NJP] = np.arange(NJP)
    for r in range(3):
        k[r, K_ROW + r] = 1.0
    f, e = np.arange(E)[None, :], np.arange(E)[:, None]
    k[:, K_ENDS:K_ENDS + 2 * E * E] = np.stack([f <= e, P * (f < e)]).reshape(1, -1)
    return c


PAIR_UNITS = [[(0, 0, 0)], [(0, 1, 0), (0, 3, 384)], [(1, 0, 0)], [(1, 1, 0), (1, 3, 384)],
              [(0, 2, 0), (1, 2, 256)]]
UNITS = [[(2 * pair + h, t, c) for h, t, c in u] for pair in range(2) for u in PAIR_UNITS]
NU = len(UNITS)
WIDE = [(QT - t) * P for t in range(QT)]
PROB_AT = {(h, t): 512 * k + c for k, u in enumerate(PAIR_UNITS) for h, t, c in u}
REDS = [len(u) if len({t for _, t, _ in u}) > 1 else 1 for u in UNITS]
RED_TO = [sum(REDS[:u + 1]) for u in range(NU)]
NRED = RED_TO[-1]
ABANK = [i % 3 for i in range(G * NU)]
ABANK[-1] = 1
SBANK = [i % 2 for i in range(G * NU)]


def before(i, banks):
    j = i - 1
    while banks[j % (G * NU)] != banks[i]:
        j -= 1
    return j


def stages(b, g):
    if isinstance(b, int):
        s = 4 * b + g
        return [0 <= s - lag < B * G for lag in range(4)] + [g == 3 and b > 0]
    return [True] * 4 + [g == 3]


def blocks(eng, step):
    for b in (0, 1):
        for g in range(G):
            step(b, g)
    with eng.Fori(2, B - 1) as b:
        for g in range(G):
            step(b, g)
    for b in (B - 1, B):
        for g in range(G):
            step(b, g)


def early(b, g, n):
    return isinstance(b, int) and 4 * b + g < n


def normalisations(b, g):
    has = [projects_next(b), not isinstance(b, int) or b >= 2]
    taken = {0: 0, 1: 1}.get(g)
    turned = {1: 0, 2: 1}.get(g)
    return [k if k is not None and has[k] else None for k in (taken, turned)]


def projects_next(b):
    return not isinstance(b, int) or b + 1 < B


def normalised(kind, b):
    return b + 1 if kind == 0 else b - 2


PREP = 11

PE_ORDER = [("scores a", 0), ("maxima", 0), ("scores a", 1), ("q rows", 0), ("scores a", 2), ("scores b", 0),
            ("k rows", 0), ("values", 0), ("scores a", 3), ("scores a", 4), ("scores b", 1), ("values", 1),
            ("scores b", 2), ("scores a", 5), ("attention", 0), ("scores b", 3), ("k all", 0), ("scores a", 6),
            ("scores b", 4), ("x", 0), ("scores a", 7), ("scores b", 5), ("values", 2), ("q all", 0), ("values", 3),
            ("v all", 0), ("scores b", 6), ("scores a", 8), ("scores b", 7), ("outputs", 0), ("projection", 0),
            ("scores b", 8), ("scores a", 9), ("scores b", 9)]

POOL_ORDER = [("keys", 0), ("select", 0), ("select", 1), ("roots", 0)]

ACT_ORDER = [("k rows", 0), ("q rows", 0), ("exp", 0), ("exp", 1), ("exp", 2), ("attention", 0), ("exp", 3),
             ("k all", 0), ("copy", 0), ("exp", 4), ("x", 0), ("exp", 5), ("q all", 0), ("outputs", 0), ("v all", 0),
             ("exp", 6), ("exp", 7), ("exp", 8), ("exp", 9)]

DVE_ORDER = [("maximum", 0), ("maxima", 0), ("maximum", 1), ("maximum", 2), ("statistics", 0), ("maximum", 3),
             ("normalise", 0), ("maximum", 4), ("maximum", 5), ("k all", 0), ("maximum", 6), ("x", 0), ("q all", 0),
             ("maximum", 7), ("maximum", 8), ("outputs", 0), ("residual", 0), ("maximum", 9)]


def tile_blocks(eng, step, begin=None):
    for lo, hi in ((0, 1), (1, 2), (2, NJBP), (NJBP, NJBP + 1), (NJBP + 1, NJB), (NJB, NJB + 1)):
        if hi - lo == 1:
            extra = begin(lo) if begin else None
            for k in range(NX if lo < NJB else 2):
                step(lo, k, extra, lo // NJBP)
        else:
            with eng.Fori(lo, hi) as jb:
                extra = begin(jb) if begin else None
                for k in range(NX):
                    step(jb, k, extra, lo // NJBP)


def program(nc, x_d, wqkv_d, wo_d, gate_d, gbias_d, wu_d, bu_d, sbu_d, wd_d, bd_d, const_d, out_d):
    with ExitStack() as ctx:
        def sb(name, shape, dt=FP32):
            return ctx.enter_context(nc.sbuf_tensor(name, shape, dt))

        def sem(name):
            return ctx.enter_context(nc.semaphore(name))

        const = sb("const", [P, C_WIDTH])
        ident = const[:, C_ID:C_ID + P]
        identb, identh = sb("identb", [P, P], BF16), sb("identh", [P, P], FP16)
        causal = sb("causal", [P, P], BF16)
        onesb = sb("onesb", [P, P], BF16)

        def col(k, n=1):
            return const[:, C_COL + k:C_COL + k + n]

        x = sb("x", [P, NT, D])
        xn = sb("xn", [P, 2, QT, D])
        x_hi = sb("x_hi", [P, T], FP16)
        x_lo = sb("x_lo", [P, T], FP16)
        stats, mv = sb("stats", [P, 2, QT, 6]), sb("mv", [P, 2, QT, 2])
        varc, rstd = sb("varc", [P, 2, QT]), sb("rstd", [P, 2, QT])
        wqkv = sb("wqkv", [P, 3 * D])
        w_hi = sb("w_hi", [P, 3 * D], FP16)
        w_lo = sb("w_lo", [P, 3 * D], FP16)
        qk_hi, qk_lo = sb("qk_hi", [P, 2, S], FP16), sb("qk_lo", [P, 2, S], FP16)
        pick = sb("pick", [P, 2, 2, H, 4, DK], FP16)
        wo = sb("wo", [P, D])
        q4 = sb("q4", [P, 2, S], FP16)
        k4 = sb("k4", [P, 2, S], FP16)
        kh = sb("kh", [P, G, HG, S], FP16)
        qf = sb("qf", [P, 2, S], FP16)
        va = sb("va", [P, QT, G, HG, 32])
        mt = sb("mt", [P, 2, QT, P], FP16)
        pr = sb("pr", [P, 2, 2, 2560])
        ot = sb("ot", [P, S])
        rec = sb("rec", [P, QT, HG])
        attn = sb("attn", [P, QT, D])
        attn_t = sb("attn_t", [P, S])

        spare = pr.rearrange("p a b c -> p (a b c)")
        spare_at = [0]

        def in_spare(*shape):
            n = 1
            for k in shape:
                n *= k
            spare_at[0] += n
            flat = spare[:, spare_at[0] - n:spare_at[0]]
            names = "abcd"[:len(shape)]
            return flat.rearrange(f"p ({' '.join(names)}) -> p {' '.join(names)}", **dict(zip(names, shape)))

        def bank(name):
            return ctx.enter_context(nc.psum_tensor(name, [P, 512], FP32))

        ps_a = [bank(f"ps_a{i}") for i in range(3)]
        ps_b = [bank(f"ps_b{i}") for i in range(2)]
        ps_o = bank("ps_o")
        ps_m = [bank(f"ps_m{i}") for i in range(2)]

        const_in, x_in, x_rest_in, w_in, out_done = (
            sem(n) for n in ("const_in", "x_in", "x_rest_in", "w_in", "out_done"))
        pool_passed, sp_passed, pick_zeroed = sem("pool_passed"), sem("sp_passed"), sem("pick_zeroed")
        dve_passed, wqkv_in = sem("dve_passed"), sem("wqkv_in")
        prep, filled = sem("prep"), sem("filled")
        bn_ready, mv_ready, var_ready, rstd_ready, xn_ready, xt_ready, xhi_ready, xlo_ready = (
            [sem(f"{n}{k}") for k in range(2)] for n in (
                "bn_ready", "mv_ready", "var_ready", "rstd_ready", "xn_ready", "xt_ready", "xhi_ready", "xlo_ready"))
        q_proj, k_proj, v_proj = sem("q_proj"), sem("k_proj"), sem("v_proj")
        scores_a, maxima_turned_ready, scores_b, values_weighted, outputs_turned_ready = (
            sem(n) for n in ("scores_a", "maxima_turned_ready", "scores_b", "values_weighted", "outputs_turned_ready"))
        v_ready, probs_ready, outputs_copied = sem("v_ready"), sem("probs_ready"), sem("outputs_copied")
        all_proj, all_hi, all_lo = ([sem(f"{n}{k}") for k in "qk"] for n in ("all_proj", "all_hi", "all_lo"))
        q4_ready, k4_ready, maxima_found, qf_ready, rec_ready, normed = (
            sem(n) for n in ("q4_ready", "k4_ready", "maxima_found", "qf_ready", "rec_ready", "normed"))
        head_keys_ready, selected = sem("head_keys_ready"), sem("selected")
        attention_turned_ready, attention_copied, output_projected_ready, x2_ready = (
            sem(n) for n in ("attention_turned_ready", "attention_copied", "output_projected_ready", "x2_ready"))
        gate_done, logits_ready, exp_ready, routing_step = (
            sem(n) for n in ("gate_done", "logits_ready", "exp_ready", "routing_step"))
        ffn_in, wu_high, wu_low, ffn_prep = (sem(n) for n in ("ffn_in", "wu_high", "wu_low", "ffn_prep"))

        NE = E + 1
        wu_hi = sb("wu_hi", [P, NE * F], FP16)
        wu_lo = sb("wu_lo", [P, NE * F], FP16)
        wu_raw = sb("wu_raw", [P, NE * F])
        xr = wu_raw[:, 0:NT * ROW].rearrange("p (t c) -> p t c", t=NT)
        wd = sb("wd", [P, NE * FC * D])
        sbu = sb("sbu", [P, FC])
        gw = sb("gw", [P, E])
        gw_hi = sb("gw_hi", [P, E], FP16)
        gw_lo = sb("gw_lo", [P, E], FP16)
        gb = sb("gb", [P, E])
        bu = sb("bu", [P, E * FC])
        bd = sb("bd", [P, NE * D])
        bpart = sb("bpart", [P, 3, D], BF16)
        brest = sb("brest", [P, 2, D])
        bd_rows = sb("bd_rows", [P, D], BF16)
        lg, sig = in_spare(NT, E), in_spare(NT, E)
        score, key, rest_of = sb("score", [P, KTOP, NT]), sb("key", [P, KTOP, NT]), in_spare(NTP, E)
        tied = in_spare(NTP, E)
        oh, ohs = in_spare(PARTS, KTOP, NTP, E), in_spare(KTOP, NTP, E)
        chosen = sb("chosen", [P, NT, E], BF16)
        beforeb, allb = sb("beforeb", [P, P], BF16), sb("allb", [P, P], BF16)
        wgt, den = sb("wgt", [P, KTOP, NT]), sb("den", [P, NT])
        over, tiles, ends = in_spare(E, NTP), sb("tiles", [P, E]), sb("ends", [P, 2, E])
        share, place = in_spare(2, E, E), in_spare(NTP, E)
        posf, pos = sb("posf", [P, PARTS, KTOP, NTP]), sb("pos", [P, PARTS, KTOP, NTP], U32)
        past, te = in_spare(NJP, E), sb("te", [P, NJP])
        te_table = sb("te_table", [P, NJ + NX + 1], I32)
        blank = sb("blank", [P, ROW])
        ids = sb("ids", [P, KTOP, NTP], I32)
        xt = in_spare(NX, ROW)
        xh, xl = sb("xh", [P, 2, P], FP16), sb("xl", [P, 2, P], FP16)
        ps_down = [ps_o, ps_a[2]]
        sh_bank = [ps_a[0], ps_a[1], ps_b[0], ps_b[1]]
        gate_bank, rank_bank, RANK = [ps_a[2], ps_m[0]], [ps_a[2], ps_m[1]], NTP * E
        act2 = in_spare(2, FC, P)
        act = kh.rearrange("p g h s -> p (g h s)").bitcast(FP32).rearrange("p (a f s) -> p a f s", a=2, f=FC)
        y = in_spare(NX, D)
        yb = in_spare(BP, QT, KTOP, D)
        x_sorted = [nc.dram_tensor(f"x_sorted{h}", (NJP * P, ROW), FP32, kind="Internal").ap() for h in range(PARTS)]
        y_token = [nc.dram_tensor(f"y_token{h}", (TP * KTOP, D), FP32, kind="Internal").ap() for h in range(PARTS)]
        blanked, ids_set = sem("blanked"), sem("ids_set")
        rows_out = [[sem(f"rows_out{h}_{c}") for c in range(2)] for h in range(PARTS)]
        row_copied = sem("row_copied")
        bias_in, bias_split = sem("bias_in"), sem("bias_split")
        ranked, routed, chosen_ready = sem("ranked"), sem("routed"), sem("chosen_ready")
        shared_up_done, shared_activated, shared_down_done, shared_added_done = (
            sem(n) for n in ("shared_up_done", "shared_activated", "shared_down_done", "shared_added_done"))
        xt_in = [sem(f"xt_in{i}") for i in range(NX)]
        y_out = [sem(f"y_out{i}") for i in range(NX)]
        tile_turned, tile_hi, tile_lo, tile_up, tile_activated, tile_down, tile_output = (
            sem(n) for n in ("tile_turned", "tile_hi", "tile_lo", "tile_up", "tile_activated", "tile_down",
                             "tile_output"))
        yb_in, yb_in_last = sem("yb_in"), [sem(f"yb_in_last{i}") for i in range(BP)]
        table_ready = sem("table_ready")
        summed, summed0 = sem("summed"), sem("summed0")

        def numbers(jb, first, n, engine):
            return nc.values_load_multi_w_load_instructions(
                te_table[0:1, bass.ds(jb * NX + first, n)], engines=[engine], min_val=0, max_val=E - 1,
                skip_runtime_bounds_check_because="an expert's number is below E by construction")[1]

        block = ctx.enter_context(nc.Block())

        @block.sync
        def _(sp):
            xv = x_d.rearrange("(t p) d -> p t d", p=P)
            sp.dma_start(x[:, 0:QT, :], xv[:, 0:QT, :]).then_inc(x_in, 16)
            sp.dma_start(const[:, :], const_d).then_inc(const_in, 16)
            sp.dma_start(wqkv[:, :], wqkv_d).then_inc(wqkv_in, 16)
            sp.dma_start(x[:, QT:NT, :], xv[:, QT:NT, :]).then_inc(x_rest_in, 16)
            sp.dma_start(wo[:, :], wo_d).then_inc(w_in, 16)
            sp.dma_start(gw[:, :], gate_d).then_inc(w_in, 16)
            sp.dma_start(gb[:, :], gbias_d.partition_broadcast(P)).then_inc(w_in, 16)
            sp.dma_start(wu_raw[:, :], wu_d).then_inc(ffn_in, 16)
            sp.dma_start(wd[:, :], wd_d).then_inc(ffn_in, 16)
            sp.dma_start(sbu[:, :], sbu_d).then_inc(ffn_in, 16)
            sp.dma_start(bu[:, :], bu_d).then_inc(bias_in, 16)
            sp.dma_start(bd[:, :], bd_d.partition_broadcast(P)).then_inc(bias_in, 16)
            sp.wait_ge(filled, 5)
            for h in range(PARTS):
                sp.dma_start(x_sorted[h].rearrange("(j p) c -> p j c", p=P),
                             blank[:, :].unsqueeze(1).to_broadcast([P, NJP, ROW])).then_inc(blanked, 16)
            xs = [x_sorted[h].rearrange("(j p) c -> p j c", p=P) for h in range(PARTS)]
            yv = [y_token[h].rearrange("(t p k) d -> p t (k d)", p=P, k=KTOP) for h in range(PARTS)]
            ov = out_d.rearrange("(t p) d -> p t d", p=P)

            def load(jb, k, h):
                j = NX * jb + k
                if not (isinstance(jb, int) and jb == 0):
                    sp.wait_ge(tile_turned, j - NX + 1)
                    sp.sem_inc(sp_passed, 1)
                    sp.wait_ge(y_out[k], 16 * jb)
                    sp.sem_inc(sp_passed, 1)
                sp.dma_start(xt[:, k, :], xs[h][:, bass.ds(j - h * NJP, 1), :].rearrange("p a c -> p (a c)"))\
                    .then_inc(xt_in[k], 16)

            def fetch(h, batch, i, ready):
                sp.dma_start(yb[:, i, :, :, :].rearrange("p t k d -> p t (k d)"),
                             yv[h][:, bass.ds(batch * QT, QT), :]).then_inc(ready, 16)

            for c in range(2):
                sp.wait_ge(rows_out[0][c], 16 * KTOP * NTP // 2)
            for k in range(NX):
                load(0, k, 0)
            with sp.Fori(1, NJBP) as jb:
                for k in range(NX):
                    load(jb, k, 0)
            for c in range(2):
                sp.wait_ge(rows_out[1][c], 16 * KTOP * NTP // 2)
            for k in range(NX):
                load(NJBP, k, 1)
            with sp.Fori(NJBP + 1, NJBP + 1 + BP) as jb:
                for k in range(NX):
                    load(jb, k, 1)
                    if k == COMBINE + QT - NX // 2:
                        sp.wait_ge(summed, (jb - NJBP) * QT)
                        sp.sem_inc(sp_passed, 1)
                        fetch(0, jb - (NJBP + 1), 0, yb_in)
            for k in range(NX):
                sp.wait_ge(y_out[k], 16 * NJB)
            for i in range(BP):
                fetch(1, i, i, yb_in_last[i])
            sp.wait_ge(summed, (BP + 1) * QT)
            sp.dma_start(ov[:, 0:NTP, :], x[:, 0:NTP, :]).then_inc(out_done, 16)
            for i in range(BP):
                sp.wait_ge(summed, (BP + 2 + i) * QT)
                ts = slice(NTP + i * QT, NTP + (i + 1) * QT)
                sp.dma_start(ov[:, ts, :], x[:, ts, :]).then_inc(out_done, 16)
            sp.wait_ge(out_done, 16 * (BP + 1))

        @block.gpsimd
        def _(pool):
            def wait_alone(semaphore, value):
                pool.wait_ge(semaphore, value)
                pool.sem_inc(pool_passed, 1)

            nc.gpsimd.memset(pick.rearrange("p a b h c d -> p (a b h c d)"), 0.0).then_inc(pick_zeroed, 1)

            def inverse_roots(kind, batch):
                n = batch + 1
                wait_alone(mv_ready[kind], QT * n)
                nc.gpsimd.tensor_scalar(varc[:, kind, :], mv[:, kind, :, 1], EPS, 1.0 / (XS * XS), ALU.add, ALU.mult)\
                    .then_inc(var_ready[kind], 1)
                wait_alone(var_ready[kind], n)
                nc.gpsimd.tensor_tensor(rstd[:, kind, :], varc[:, kind, :], col(K_POW, QT), ALU.pow)\
                    .then_inc(rstd_ready[kind], 1)

            pool.wait_ge(const_in, 16)
            inverse_roots(0, 0)

            nc.gpsimd.memset(mt.rearrange("p a t c -> p (a t c)"), 0.0).then_inc(filled, 1)
            nc.gpsimd.memset(va.rearrange("p t g h c -> p (t g h c)"), 0.0).then_inc(filled, 1)
            pool.wait_ge(filled, 2)
            nc.gpsimd.memset(va.rearrange("p t g h c -> p (t g h) c")[:, :, DK:DK + 1], 1.0).then_inc(filled, 1)
            nc.gpsimd.memset(blank[:, 0:D], 0.0).then_inc(filled, 1)
            nc.gpsimd.iota(blank[:, D:ROW].bitcast(I32), pattern=[[0, 1]], base=int(NOWHERE), channel_multiplier=0)\
                .then_inc(filled, 1)
            nc.gpsimd.memset(allb[:, :], 1.0).then_inc(filled, 1)
            nc.gpsimd.iota(ids.rearrange("p k t -> p (k t)"), pattern=[[1, KTOP], [KTOP * P, NTP]], base=0,
                           channel_multiplier=KTOP).then_inc(filled, 1)

            def step(b, g):
                s = 4 * b + g
                project, _, scores, _, _ = stages(b, g)

                def one_head_keys():
                    wait_alone(k4_ready, s + 1)
                    if not early(b, g, 4):
                        wait_alone(scores_b, (s - 3) * NU)
                    for j in range(HG):
                        nc.gpsimd.tensor_scalar(kh[:, g, j, :], k4[:, g % 2, :], col(K_MASK + j), col(K_NEG + j),
                                                ALU.mult, ALU.add).then_inc(head_keys_ready, 1)

                def select(pair):
                    n = s - 2
                    row = pr[:, g % 2, pair, :]
                    wait_alone(probs_ready, n * NU + 5 * (pair + 1))
                    full = row[:, 0:2048].rearrange("p (a b c) -> p a b c", a=2, b=2)[:, :, :, 0:P]
                    third = row[:, 0:2048].rearrange("p (a c) -> p a c", a=2)[:, :, 896:1024]
                    second = row[:, 2048:2560].rearrange("p (a c) -> p a c", a=2)[:, :, 0:P]
                    for d, pattern in ((full, [[0, 2], [0, 2], [1, P]]), (third, [[0, 2], [1, P]]),
                                       (second, [[0, 2], [1, P]])):
                        nc.gpsimd.affine_select(out=d, in_=d, pattern=pattern, compare_op=ALU.is_ge, fill=0.0, base=0,
                                                channel_multiplier=-1).then_inc(selected, 1)

                taken, _ = normalisations(b, g)
                for what, u in POOL_ORDER:
                    if what == "keys" and project:
                        one_head_keys()
                    elif what == "roots" and taken is not None:
                        inverse_roots(taken, normalised(taken, b))
                    elif what == "select" and scores:
                        select(u)

            blocks(pool, step)
            inverse_roots(1, B - 1)
            pool.wait_ge(blanked, 16 * PARTS)
            pool.wait_ge(filled, 7)

            sets = [0]

            def places_set(h, k, c):
                if k:
                    pool.wait_ge(rows_out[h][c], 16 * NTP // 2)
                ts = slice(h * NTP + c * NTP // 2, h * NTP + (c + 1) * NTP // 2)
                nc.gpsimd.tensor_copy(xr[:, ts, D].bitcast(I32), ids[:, k, c * NTP // 2:(c + 1) * NTP // 2])\
                    .then_inc(ids_set, 1)
                sets[0] += 1
                pool.wait_ge(ids_set, sets[0])
                if not k and not c:
                    pool.wait_ge(routed, h + 1)
                    pool.wait_ge(row_copied, BP * (h + 1))

            def scatter(h, k, c, t):
                t += c * NTP // 2
                nc.gpsimd.indirect_dma_start(x_sorted[h], bass.IndirectOffsetOnAxis(ap=pos[:, h, k, t:t + 1], axis=0),
                                             xr[:, h * NTP + t, :], None).then_inc(rows_out[h][c], 16)

            quarters = [(k, c) for k in range(KTOP) for c in range(2)]
            for k, c in quarters:
                places_set(0, k, c)
                for t in range(NTP // 2):
                    scatter(0, k, c, t)
            assert NTP // 2 == NX

            def scatter_quarter(n, k):
                if k == 0:
                    places_set(1, *quarters[n])
                scatter(1, *quarters[n], k)

            for n in range(2):
                for k in range(NX):
                    scatter_quarter(n, k)

            def send(jb, k, _, h):
                if isinstance(jb, int) and jb < 2:
                    scatter_quarter(2 + jb, k)
                if isinstance(jb, int) and not 0 <= NX * jb + k - 2 < NJ:
                    return
                j, q = NX * jb + k - 2, (k - 2) % NX
                if isinstance(jb, int):
                    h = j // NJP
                wait_alone(tile_output, j + 1)
                nc.gpsimd.indirect_dma_start(
                    y_token[h], bass.IndirectOffsetOnAxis(ap=xt[:, q, D:ROW].bitcast(U32), axis=0), y[:, q, :], None,
                    bounds_check=TP * KTOP - 1, oob_is_err=False).then_inc(y_out[q], 16)

            tile_blocks(pool, send)

        @block.scalar
        def _(act_e):
            def high_part_of_x(kind, batch):
                act_e.wait_ge(xt_ready[kind], batch + 1)
                nc.scalar.activation(x_hi[:, bass.ds(batch * S, S)], ps_m[1][:, :], ACT.Copy)\
                    .then_inc(xhi_ready[kind], 1)

            def high_part_of_all(a, batch):
                act_e.wait_ge(all_proj[a], batch + 1)
                nc.scalar.activation(qk_hi[:, a, :], ps_m[a][:, :], ACT.Copy, scale=1.0 / (XS * WS))\
                    .then_inc(all_hi[a], 1)

            def shared_act(b, par):
                for f in range(FC):
                    act_e.wait_ge(shared_up_done, FC * b + f + 1)
                    if not early(b, 0, 2 * G):
                        act_e.wait_ge(shared_down_done, b - 1)
                    nc.scalar.activation(act[:, par, f, :], sh_bank[f][:, :], ACT.Gelu, bias=sbu[:, f:f + 1],
                                         scale=1.0 / (XS * US)).then_inc(shared_activated, 1)

            def gate_exp(h):
                ts = slice(h * NTP, (h + 1) * NTP)
                act_e.wait_ge(logits_ready, h + 1)
                nc.scalar.activation(sig[:, ts, :], lg[:, ts, :], ACT.Exp, scale=-1.0).then_inc(exp_ready, 1)

            def rows_copied(batch):
                act_e.wait_ge(xn_ready[1], QT * (batch + 1))
                nc.scalar.activation(xr[:, bass.ds(batch * QT, QT), 0:D], xn[:, 1, :, :], ACT.Copy)\
                    .then_inc(row_copied, 1)

            high_part_of_x(0, 0)
            high_part_of_all(0, 0)
            high_part_of_all(1, 0)

            def step(b, g):
                s = 4 * b + g
                project, _, scores, values, output = stages(b, g)
                i0 = ((g - 2) % G) * NU

                def probs(u):
                    n = s - 2
                    act_e.wait_ge(scores_b, n * NU + u + 1)
                    if u == 0 and not early(b, g, 4):
                        act_e.wait_ge(values_weighted, n - 1)
                    pair, k = divmod(u, 5)
                    nc.scalar.activation(pr[:, g % 2, pair, 512 * k:512 * (k + 1)], ps_b[SBANK[i0 + u]][:, :],
                                         ACT.Exp, scale=float(DK) ** -0.5).then_inc(probs_ready, 1)

                def queries():
                    act_e.wait_ge(q_proj, s + 1)
                    if not early(b, g, 2):
                        act_e.wait_ge(qf_ready, s - 1)
                    nc.scalar.activation(q4[:, g % 2, :], ps_m[0][:, :], ACT.Copy).then_inc(q4_ready, 1)

                def keys():
                    act_e.wait_ge(k_proj, s + 1)
                    if not early(b, g, 2):
                        act_e.wait_ge(head_keys_ready, HG * (s - 1))
                    nc.scalar.activation(k4[:, g % 2, :], ps_m[1][:, :], ACT.Copy).then_inc(k4_ready, 1)

                def values_out():
                    act_e.wait_ge(v_proj, b + 1)
                    if not early(b, g, 4):
                        act_e.wait_ge(values_weighted, s - 2)
                    else:
                        act_e.wait_ge(filled, 3)
                    nc.scalar.activation(va.rearrange("p t g h c -> p (t g h) c")[:, :, 0:DK],
                                         ps_m[0][:, :].rearrange("p (a d) -> p a d", d=DK),
                                         ACT.Copy, scale=1.0 / (XS * WS)).then_inc(v_ready, 1)

                def outputs_out():
                    n = s - 3
                    act_e.wait_ge(values_weighted, n + 1)
                    if not early(b, g, 4):
                        act_e.wait_ge(outputs_turned_ready, n)
                    nc.scalar.activation(ot[:, :], ps_o[:, :], ACT.Copy).then_inc(outputs_copied, 1)

                _, turned = normalisations(b, g)
                for what, u in ACT_ORDER:
                    if what == "exp" and scores:
                        probs(u)
                    elif what == "q rows" and project:
                        queries()
                    elif what == "k rows" and project:
                        keys()
                    elif what in ("q all", "k all") and projects_next(b) and g == G - 1:
                        high_part_of_all("qk".index(what[0]), b + 1)
                    elif what == "v all" and project and g == G - 2:
                        values_out()
                    elif what == "attention" and output:
                        act_e.wait_ge(attention_turned_ready, b)
                        nc.scalar.activation(attn_t[:, :], ps_m[0][:, :], ACT.Copy).then_inc(attention_copied, 1)
                    elif what == "outputs" and values:
                        outputs_out()
                    elif what == "x" and turned is not None:
                        high_part_of_x(turned, normalised(turned, b))
                    elif what == "copy" and turned == 1:
                        rows_copied(normalised(turned, b))
                if isinstance(b, int) and s == B * G + 2:
                    gate_exp(0)
                if early(b, g, 7) and s >= 3:
                    act_e.wait_ge(ffn_in, 48)
                    cols = slice((s - 3) * NE * F // 4, (s - 2) * NE * F // 4)
                    nc.scalar.activation(wu_hi[:, cols], wu_raw[:, cols], ACT.Copy, scale=US).then_inc(wu_high, 1)

            blocks(act_e, step)
            shared_act(0, 0)
            high_part_of_x(1, B - 1)
            shared_act(1, 1)
            rows_copied(B - 1)
            gate_exp(1)
            with act_e.Fori(1, B // 2) as m:
                shared_act(2 * m, 0)
                shared_act(2 * m + 1, 1)

            def tile_act(jb, k, e, h):
                j = NX * jb + k
                first = isinstance(jb, int) and jb == 0
                if not isinstance(jb, int) or j < NJ:
                    act_e.wait_ge(tile_turned, j + 1)
                    if not (first and k < 2):
                        act_e.wait_ge(tile_up, j - 1)
                    nc.scalar.activation(xh[:, k % 2, :], ps_m[k % 2][:, 0:P], ACT.Copy).then_inc(tile_hi, 1)
                if not isinstance(jb, int) or 0 <= j - 1 < NJ:
                    act_e.wait_ge(tile_up, j)
                    if not (first and k < 3):
                        act_e.wait_ge(tile_down, j - 2)
                    q = (k - 1) % 2
                    for f in range(FC):
                        ins = nc.scalar.activation(act2[:, q, f, :], ps_a[q][:, f * P:(f + 1) * P], ACT.Gelu,
                                                   bias=bu[:, bass.ds(e[k] * FC + f, 1)], scale=1.0 / (XS * US))
                    ins.then_inc(tile_activated, 1)

            act_e.wait_ge(table_ready, 1 + PARTS)
            act_e.wait_ge(bias_in, 32)
            tile_blocks(act_e, tile_act, lambda jb: numbers(jb, 1, NX, mybir.EngineType.Activation))

        @block.vector
        def _(dve):
            v = nc.vector

            def statistics(kind, batch):
                for i in range(QT):
                    t = batch * QT + i
                    v.bn_stats(stats[:, kind, i, :], x[:, bass.ds(t, 1), :]).then_inc(bn_ready[kind], 1)
                dve.wait_ge(bn_ready[kind], QT * (batch + 1))
                dve.sem_inc(dve_passed, 1)
                for i in range(QT):
                    v.bn_aggr(mv[:, kind, i, :], stats[:, kind, i, :]).then_inc(mv_ready[kind], 1)

            def normalise(kind, batch):
                dve.wait_ge(rstd_ready[kind], batch + 1)
                for i in range(QT):
                    t = batch * QT + i
                    v.tensor_scalar(xn[:, kind, i, :], x[:, bass.ds(t, 1), :], mv[:, kind, i, 0:1],
                                    rstd[:, kind, i:i + 1], ALU.subtract, ALU.mult).then_inc(xn_ready[kind], 1)

            def low_part_of_x(kind, batch):
                dve.wait_ge(xhi_ready[kind], batch + 1)
                cols = bass.ds(batch * S, S)
                v.tensor_tensor(x_lo[:, cols], ps_m[1][:, :], x_hi[:, cols], ALU.subtract)\
                    .then_inc(xlo_ready[kind], 1)

            def weights_prepared():
                dve.wait_ge(wqkv_in, 16)
                v.tensor_scalar(w_hi[:, :], wqkv[:, :], WS, None, ALU.mult).then_inc(prep, 1)
                dve.wait_ge(prep, 1)
                v.scalar_tensor_tensor(w_lo[:, :], wqkv[:, :], WS, w_hi[:, :], ALU.mult, ALU.subtract)\
                    .then_inc(prep, 1)

            def biases_split():
                dve.wait_ge(bias_in, 32)
                rest = bd[:, E * D:]
                for r in range(3):
                    v.tensor_copy(bpart[:, r, :], rest).then_inc(bias_split, 1)
                    dve.wait_ge(bias_split, 3 * r + 1)
                    if r == 0:
                        v.tensor_scalar(bd_rows[:, :], bpart[:, r, :], col(K_ROW), None, ALU.mult)\
                            .then_inc(bias_split, 1)
                    else:
                        v.scalar_tensor_tensor(bd_rows[:, :], bpart[:, r, :], col(K_ROW + r), bd_rows[:, :],
                                               ALU.mult, ALU.add).then_inc(bias_split, 1)
                    if r < 2:
                        v.tensor_tensor(brest[:, r, :], rest, bpart[:, r, :], ALU.subtract).then_inc(bias_split, 1)
                        dve.wait_ge(bias_split, 3 * r + 3)
                        rest = brest[:, r, :]

            def low_part_of_all(a, batch):
                dve.wait_ge(all_hi[a], batch + 1)
                v.scalar_tensor_tensor(qk_lo[:, a, :], ps_m[a][:, :], 1.0 / (XS * WS), qk_hi[:, a, :], ALU.mult,
                                       ALU.subtract).then_inc(all_lo[a], 1)

            dve.wait_ge(x_in, 16)
            statistics(0, 0)
            weights_prepared()
            normalise(0, 0)
            dve.wait_ge(pick_zeroed, 1)
            rows = ident.rearrange("p (h d) -> p h d", h=H)
            for a, places in ((0, (0, 0, 1)), (1, (0, 1, 0))):
                for c, part in enumerate(places):
                    v.tensor_copy(pick[:, a, part, :, c, :], rows).then_inc(prep, 1)
            for dst, src in ((identb, C_ID), (identh, C_ID), (causal, C_CAUSAL)):
                v.tensor_copy(dst[:, :], const[:, src:src + P]).then_inc(prep, 1)
            assert PREP == 2 + 6 + 3
            low_part_of_x(0, 0)
            low_part_of_all(0, 0)
            low_part_of_all(1, 0)

            def last_weights():
                dve.wait_ge(w_in, 48)
                v.tensor_scalar(gw_hi[:, :], gw[:, :], GS, None, ALU.mult).then_inc(ffn_prep, 1)
                for dst, src in ((onesb, C_ONES), (beforeb, C_BEFORE)):
                    v.tensor_copy(dst[:, :], const[:, src:src + P]).then_inc(ffn_prep, 1)
                dve.wait_ge(ffn_prep, 1)
                v.scalar_tensor_tensor(gw_lo[:, :], gw[:, :], GS, gw_hi[:, :], ALU.mult, ALU.subtract)\
                    .then_inc(ffn_prep, 1)
                biases_split()

            def low_up_weights(piece):
                dve.wait_ge(wu_high, piece + 1)
                cols = slice(piece * NE * F // 4, (piece + 1) * NE * F // 4)
                v.scalar_tensor_tensor(wu_lo[:, cols], wu_raw[:, cols], US, wu_hi[:, cols], ALU.mult, ALU.subtract)\
                    .then_inc(wu_low, 1)

            def add_residual(b):
                dve.wait_ge(output_projected_ready, b)
                xb = x[:, bass.ds((b - 1) * QT, QT), :].rearrange("p t d -> p (t d)")
                v.tensor_tensor(xb, ps_m[1][:, :], xb, ALU.add).then_inc(x2_ready, 1)

            count = [0]

            def then(ins):
                ins.then_inc(routing_step, 1)
                count[0] += 1
                dve.wait_ge(routing_step, count[0])

            def gate_scores(h):
                ts = slice(h * NTP, (h + 1) * NTP)
                dve.wait_ge(gate_done, h + 1)
                v.scalar_tensor_tensor(lg[:, ts, :], gate_bank[h][:, 0:NTP * E].rearrange("p (t e) -> p t e", e=E),
                                       1.0 / (XS * GS), gb[:, :].unsqueeze(1).to_broadcast([P, NTP, E]), ALU.mult,
                                       ALU.add).then_inc(logits_ready, 1)
                dve.wait_ge(exp_ready, h + 1)
                then(v.tensor_scalar(sig[:, ts, :], sig[:, ts, :], 1.0, None, ALU.add))
                then(v.reciprocal(sig[:, ts, :], sig[:, ts, :]))

            def per_expert(ap):
                return ap.unsqueeze(1).to_broadcast([P, NTP, E])

            def per_token(ap, n=E):
                return ap.unsqueeze(2).to_broadcast([P, NTP, n])

            def two_best(h):
                ts = slice(h * NTP, (h + 1) * NTP)
                left = sig[:, ts, :]
                for r in range(KTOP):
                    if r:
                        then(v.scalar_tensor_tensor(rest_of[:, :, :], oh[:, h, 0, :, :], -2.0, left, ALU.mult, ALU.add))
                        left = rest_of[:, :, :]
                    then(v.tensor_reduce(score[:, r, ts], left, AX, ALU.max))
                    then(v.tensor_tensor(tied[:, :, :], left, per_token(score[:, r, ts]), ALU.is_equal))
                    then(v.tensor_tensor(tied[:, :, :], tied[:, :, :], per_expert(col(K_REV, E)), ALU.mult))
                    then(v.tensor_reduce(key[:, r, ts], tied[:, :, :], AX, ALU.max))
                    then(v.tensor_tensor(oh[:, h, r, :, :], per_expert(col(K_REV, E)), per_token(key[:, r, ts]),
                                         ALU.is_equal))
                v.tensor_tensor(chosen[:, ts, :], oh[:, h, 0, :, :], oh[:, h, 1, :, :], ALU.add)\
                    .then_inc(chosen_ready, 1)

            def two_weights(h):
                ts = slice(h * NTP, (h + 1) * NTP)
                then(v.tensor_tensor(den[:, ts], score[:, 0, ts], score[:, 1, ts], ALU.add))
                then(v.tensor_scalar(den[:, ts], den[:, ts], 1e-6, None, ALU.add))
                then(v.reciprocal(den[:, ts], den[:, ts]))
                then(v.tensor_tensor(wgt[:, :, ts], score[:, :, ts],
                                     den[:, ts].unsqueeze(1).to_broadcast([P, KTOP, NTP]), ALU.mult))

            def places(h):
                dve.wait_ge(ranked, h + 1)
                rank = rank_bank[h][:, RANK:RANK + NTP * E].rearrange("p (t e) -> p t e", e=E)
                total = rank_bank[h][:, RANK + NTP * E:RANK + NTP * E + E]
                then(v.scalar_tensor_tensor(over[:, :, :], total.unsqueeze(2).to_broadcast([P, E, NTP]), 1.0 / P,
                                            col(K_TILE, NTP).unsqueeze(1).to_broadcast([P, E, NTP]), ALU.mult,
                                            ALU.is_gt))
                then(v.tensor_reduce(tiles[:, :], over[:, :, :], AX, ALU.add))
                then(v.tensor_tensor(share[:, :, :, :].rearrange("p a e f -> p (a e) f"),
                                     tiles[:, :].unsqueeze(1).to_broadcast([P, 2 * E, E]),
                                     col(K_ENDS, 2 * E * E).rearrange("p (a f) -> p a f", f=E), ALU.mult))
                then(v.tensor_reduce(ends[:, :, :], share[:, :, :, :], AX, ALU.add))
                then(v.tensor_tensor(place[:, :, :], rank, per_expert(ends[:, 1, :]), ALU.add))
                for r in range(KTOP):
                    ins = v.tensor_tensor(ohs[:, r, :, :], oh[:, h, r, :, :], place[:, :, :], ALU.mult)
                then(ins)
                then(v.tensor_reduce(posf[:, h, :, :], ohs[:, :, :, :], AX, ALU.add))
                v.tensor_copy(pos[:, h, :, :], posf[:, h, :, :]).then_inc(routed, 1)
                then(v.tensor_tensor(past[:, :, :], col(K_TILE, NJP).unsqueeze(2).to_broadcast([P, NJP, E]),
                                     ends[:, 0, :].unsqueeze(1).to_broadcast([P, NJP, E]), ALU.is_ge))
                then(v.tensor_reduce(te[:, :], past[:, :, :], AX, ALU.add))
                dve.wait_ge(table_ready, 1)
                v.tensor_scalar(te_table[:, h * NJP + 2:(h + 1) * NJP + 2], te[:, :], float(E - 1), None, ALU.min)\
                    .then_inc(table_ready, 1)

            def shared_added(b, par):
                dve.wait_ge(shared_down_done, b + 1)
                xb = x[:, bass.ds(b * QT, QT), :].rearrange("p t d -> p (t d)")
                v.scalar_tensor_tensor(xb, ps_down[par][:, :], 0.1, xb, ALU.mult, ALU.add)\
                    .then_inc(shared_added_done, 1)

            def step(b, g):
                s = 4 * b + g
                project, maxima, scores, values, output = stages(b, g)
                first = isinstance(b, int) and b == 0

                def maximum(u):
                    n, par = s - 1, (g - 1) % 2
                    dve.wait_ge(scores_a, n * NU + u + 1)
                    if u == 0 and not (first and g < 3):
                        dve.wait_ge(maxima_turned_ready, n - 1)
                    elif u == 0:
                        dve.wait_ge(filled, 1)
                    src = ps_a[ABANK[(g - 1) % G * NU + u]]
                    h, t, _ = UNITS[u][0]
                    at = 32 * h + 3 * DK
                    if REDS[u] == 1 and len(UNITS[u]) == 2:
                        v.tensor_reduce(mt[:, par, QT - 1 - t, at:at + 33:32],
                                        src[:, :].rearrange("p (a c) -> p a c", a=2), AX, ALU.max)\
                            .then_inc(maxima_found, 1)
                        return
                    for h, t, c in UNITS[u]:
                        v.tensor_reduce(mt[:, par, QT - 1 - t, at:at + 1], src[:, c:c + WIDE[t]], AX, ALU.max)\
                            .then_inc(maxima_found, 1)

                def queries_with_maxima():
                    n, par = s - 2, g % 2
                    dve.wait_ge(maxima_turned_ready, n + 1)
                    dve.wait_ge(q4_ready, n + 1)
                    if not first:
                        dve.wait_ge(scores_b, NU * (n - 1))
                    v.tensor_tensor(qf[:, par, :], q4[:, par, :], ps_m[1][:, :], ALU.add).then_inc(qf_ready, 1)

                def normalise_outputs():
                    n, gi = s - 3, (g - 3) % G
                    dve.wait_ge(outputs_turned_ready, n + 1)
                    o = ps_m[0][:, :].rearrange("p (t h c) -> p t h c", t=QT, h=HG)
                    if not first:
                        dve.wait_ge(normed, n)
                    v.reciprocal(rec[:, :, :], o[:, :, :, DK]).then_inc(rec_ready, 1)
                    dve.wait_ge(rec_ready, n + 1)
                    out = attn[:, :, gi * 32:gi * 32 + 32].rearrange("p t (h d) -> p t h d", h=HG)
                    v.tensor_tensor(out, o[:, :, :, 0:DK],
                                    rec[:, :, :].unsqueeze(3).to_broadcast([P, QT, HG, DK]), ALU.mult)\
                        .then_inc(normed, 1)

                taken, turned = normalisations(b, g)
                for what, u in DVE_ORDER:
                    if what == "maximum" and maxima:
                        maximum(u)
                    elif what == "maxima" and scores:
                        queries_with_maxima()
                    elif what in ("q all", "k all") and projects_next(b) and g == G - 1:
                        low_part_of_all("qk".index(what[0]), b + 1)
                    elif what == "residual" and output:
                        add_residual(b)
                    elif what == "outputs" and values:
                        normalise_outputs()
                    elif what == "statistics" and taken is not None:
                        if taken == 1:
                            dve.wait_ge(x2_ready, b - 1)
                        elif early(b, g, 1):
                            dve.wait_ge(x_rest_in, 16)
                        statistics(taken, normalised(taken, b))
                    elif what == "normalise" and turned is not None:
                        normalise(turned, normalised(turned, b))
                    elif what == "x" and turned is not None:
                        low_part_of_x(turned, normalised(turned, b))
                if isinstance(b, int) and s == B * G + 2:
                    gate_scores(0)
                    two_best(0)
                if isinstance(b, int) and s == 2:
                    last_weights()
                if early(b, g, 8) and s >= 4:
                    low_up_weights(s - 4)

            v.memset(te_table[:, :], 0).then_inc(table_ready, 1)
            blocks(dve, step)
            dve.wait_ge(x2_ready, B)
            statistics(1, B - 1)
            normalise(1, B - 1)
            places(0)
            two_weights(0)
            low_part_of_x(1, B - 1)
            gate_scores(1)
            shared_added(0, 0)
            two_best(1)
            two_weights(1)
            shared_added(1, 1)
            places(1)
            with dve.Fori(1, B // 2) as m:
                shared_added(2 * m, 0)
                shared_added(2 * m + 1, 1)

            def add_expert(r, t, i, q):
                xq = x[:, bass.ds(t, 1), :].rearrange("p a d -> p (a d)")
                if r:
                    dve.wait_ge(summed0, t + 1)
                v.scalar_tensor_tensor(xq, yb[:, i, q, r, :], wgt[:, r, bass.ds(t, 1)], xq, ALU.mult, ALU.add)\
                    .then_inc(summed if r else summed0, 1)

            def tile_parts(jb, k, e, h):
                j = NX * jb + k
                first = isinstance(jb, int) and jb == 0
                if not isinstance(jb, int) or j < NJ:
                    dve.wait_ge(tile_hi, j + 1)
                    if not (first and k < 2):
                        dve.wait_ge(tile_up, j - 1)
                    if not (first and k < 3):
                        dve.wait_ge(tile_output, j - 2)
                    v.tensor_tensor(xl[:, k % 2, :], ps_m[k % 2][:, 0:P], xh[:, k % 2, :], ALU.subtract)\
                        .then_inc(tile_lo, 1)
                if isinstance(jb, int) and jb == NJBP and k == 0:
                    dve.sem_inc(summed, QT)
                elif not isinstance(jb, int) and h == 1 and COMBINE <= k < COMBINE + QT:
                    if k == COMBINE:
                        dve.wait_ge(yb_in, 16 * (jb - NJBP))
                    for r in range(KTOP):
                        add_expert(r, (jb - (NJBP + 1)) * QT + k - COMBINE, 0, k - COMBINE)
                if not isinstance(jb, int) or 0 <= j - 2 < NJ:
                    dve.wait_ge(tile_down, j - 1)
                    q = (k - 2) % NX
                    sent = jb if k >= 2 else jb - 1
                    if not isinstance(jb, int) or sent > 0:
                        dve.wait_ge(y_out[q], 16 * sent)
                    v.tensor_tensor(y[:, q, :], ps_down[k % 2][:, 0:D], bd[:, bass.ds(e[k] * D, D)], ALU.add)\
                        .then_inc(tile_output, 1)

            dve.wait_ge(table_ready, 1 + PARTS)
            tile_blocks(dve, tile_parts, lambda jb: numbers(jb, 0, NX, mybir.EngineType.DVE))
            for i in range(BP):
                dve.wait_ge(yb_in_last[i], 16)
                for r in range(KTOP):
                    for q in range(QT):
                        add_expert(r, (BP + i) * QT + q, i, q)

        @block.tensor
        def _(pe):
            mm = nc.tensor.matmul

            def turned(kind, batch):
                pe.wait_ge(xn_ready[kind], QT * (batch + 1))
                for i in range(QT):
                    last = nc.tensor.transpose(ps_m[1][:, i * P:(i + 1) * P], xn[:, kind, i, :], ident)
                last.then_inc(xt_ready[kind], 1)

            pe.wait_ge(const_in, 16)
            turned(0, 0)
            pe.wait_ge(prep, PREP)

            def project_all(a, batch):
                xs, ws = bass.ds(batch * S, S), slice(a * D, (a + 1) * D)
                mm(ps_m[a][:, :], w_hi[:, ws], x_hi[:, xs], start=True, stop=False)
                mm(ps_m[a][:, :], w_hi[:, ws], x_lo[:, xs], start=False, stop=False)
                mm(ps_m[a][:, :], w_lo[:, ws], x_hi[:, xs], start=False, stop=True).then_inc(all_proj[a], 1)

            pe.wait_ge(xlo_ready[0], 1)
            project_all(0, 0)
            project_all(1, 0)

            def pick_into(a, g):
                hi = pick[:, a, 0, g * HG:(g + 1) * HG, :, :].rearrange("p h r d -> p (h r d)")
                lo = pick[:, a, 1, g * HG:(g + 1) * HG, :, :].rearrange("p h r d -> p (h r d)")
                mm(ps_m[a][:, :], hi, qk_hi[:, a, :], start=True, stop=False)
                return mm(ps_m[a][:, :], lo, qk_lo[:, a, :], start=False, stop=True)

            def project_q(b, g, s):
                if g == 0:
                    pe.wait_ge(all_lo[0], b + 1)
                if not early(b, g, 4):
                    pe.wait_ge(normed, s - 3)
                elif g == G - 1:
                    pe.wait_ge(v_ready, 1)
                elif g:
                    pe.wait_ge(q4_ready, s)
                pick_into(0, g).then_inc(q_proj, 1)

            def project_k(b, g, s):
                if g == 0:
                    pe.wait_ge(all_lo[1], b + 1)
                if not early(b, g, 2):
                    pe.wait_ge(qf_ready, s - 1)
                elif g:
                    pe.wait_ge(k4_ready, s)
                pick_into(1, g).then_inc(k_proj, 1)

            def project_v(b, s):
                pe.wait_ge(q4_ready, s + 1)
                for i in range(QT):
                    xs = bass.ds(b * S + i * P, P)
                    dst = ps_m[0][:, i * P:(i + 1) * P]
                    mm(dst, x_hi[:, xs], w_hi[:, 2 * D:3 * D], start=True, stop=False)
                    mm(dst, x_hi[:, xs], w_lo[:, 2 * D:3 * D], start=False, stop=False)
                    last = mm(dst, x_lo[:, xs], w_hi[:, 2 * D:3 * D], start=False, stop=True)
                last.then_inc(v_proj, 1)

            def gate(h):
                for t in range(h * NTP, (h + 1) * NTP):
                    xs = slice(t * P, (t + 1) * P)
                    dst = gate_bank[h][:, (t - h * NTP) * E:(t - h * NTP + 1) * E]
                    mm(dst, x_hi[:, xs], gw_hi[:, :], start=True, stop=False)
                    mm(dst, x_hi[:, xs], gw_lo[:, :], start=False, stop=False)
                    last = mm(dst, x_lo[:, xs], gw_hi[:, :], start=False, stop=True)
                last.then_inc(gate_done, 1)

            def ranks(h):
                pe.wait_ge(chosen_ready, h + 1)
                at, dst = RANK, rank_bank[h]
                ch = chosen[:, h * NTP:(h + 1) * NTP, :].rearrange("p t e -> p (t e)")
                mm(dst[:, at:at + NTP * E], beforeb[:, :], ch, start=True, stop=False)
                for back in range(1, NTP):
                    n = (NTP - back) * E
                    mm(dst[:, at + back * E:at + NTP * E], allb[:, :], ch[:, 0:n], start=False,
                       stop=(back == NTP - 1))
                for t in range(NTP):
                    last = mm(dst[:, at + NTP * E:at + NTP * E + E], allb[:, :], ch[:, t * E:(t + 1) * E],
                              start=(t == 0), stop=(t == NTP - 1))
                last.then_inc(ranked, 1)

            def shared_up(b):
                xs = bass.ds(b * S, S)
                for f in range(FC):
                    if not early(b, 0, G):
                        pe.wait_ge(shared_activated, FC * (b - 1) + f + 1)
                    ws = slice(E * F + f * P, E * F + (f + 1) * P)
                    mm(sh_bank[f][:, :], wu_hi[:, ws], x_hi[:, xs], start=True, stop=False)
                    mm(sh_bank[f][:, :], wu_hi[:, ws], x_lo[:, xs], start=False, stop=False)
                    mm(sh_bank[f][:, :], wu_lo[:, ws], x_hi[:, xs], start=False, stop=True).then_inc(shared_up_done, 1)

            def shared_down(b, par):
                pe.wait_ge(shared_activated, FC * (b + 1))
                if not early(b, 0, 2 * G):
                    pe.wait_ge(shared_added_done, b - 1)
                for i in range(QT):
                    dst = ps_down[par][:, i * P:(i + 1) * P]
                    for f in range(FC):
                        ws = slice((E * FC + f) * D, (E * FC + f + 1) * D)
                        mm(dst, act[:, par, f, i * P:(i + 1) * P], wd[:, ws], start=(f == 0), stop=False)
                    last = mm(dst, onesb[:, :], bd_rows[:, :], start=False, stop=True)
                last.then_inc(shared_down_done, 1)

            def step(b, g):
                s = 4 * b + g
                project, maxima, scores, values, output = stages(b, g)
                def a_scores(u):
                    n, gi, par = s - 1, (g - 1) % G, (g - 1) % 2
                    if u == 0:
                        pe.wait_ge(q4_ready, n + 1)
                        pe.wait_ge(head_keys_ready, HG * (n + 1))
                    i0 = gi * NU + u
                    prev = before(i0, ABANK)
                    if prev >= 0 or not early(b, g, 4):
                        pe.wait_ge(maxima_found, NRED * (n - gi + prev // NU) + RED_TO[prev % NU])
                    dst = ps_a[ABANK[i0]]
                    for h, t, c in UNITS[u]:
                        i = QT - 1 - t
                        w = WIDE[t]
                        mm(dst[:, c:c + w], q4[:, par, i * P:(i + 1) * P], kh[:, gi, h, 0:w], start=True, stop=False)
                        last = mm(dst[:, c + w - P:c + w], identb[:, :], causal[:, :], start=False, stop=True)
                    last.then_inc(scores_a, 1)

                def b_scores(u):
                    n, gi, par = s - 2, (g - 2) % G, g % 2
                    if u == 0:
                        pe.wait_ge(qf_ready, n + 1)
                    i0 = gi * NU + u
                    prev = before(i0, SBANK)
                    if prev >= 0 or not early(b, g, 4):
                        pe.wait_ge(probs_ready, NU * (n - gi) + prev + 1)
                    dst = ps_b[SBANK[i0]]
                    for h, t, c in UNITS[u]:
                        last = mm(dst[:, c:c + WIDE[t]], kh[:, gi, h, t * P:(t + 1) * P], qf[:, par, t * P:S],
                                  start=True, stop=True)
                    last.then_inc(scores_b, 1)

                def weighted_values(t):
                    n, gi, par = s - 3, (g - 3) % G, (g - 3) % 2
                    if t == 0:
                        pe.wait_ge(probs_ready, NU * (n + 1))
                        pe.wait_ge(selected, 6 * (n + 1))
                        pe.wait_ge(v_ready, b + 1 if g == G - 1 else b)
                        if not early(b, g, 4):
                            pe.wait_ge(outputs_copied, n)
                    for h in range(HG):
                        at = PROB_AT[(h % 2, t)]
                        last = mm(ps_o[32 * h:32 * h + 32, t * P:S], va[:, t, gi, h, :],
                                  pr[:, par, h // 2, at:at + WIDE[t]], start=(t == 0), stop=(t == QT - 1))
                    if t == QT - 1:
                        last.then_inc(values_weighted, 1)

                def outputs_turned():
                    n = s - 3
                    pe.wait_ge(outputs_copied, n + 1)
                    if projects_next(b) and g == G - 1:
                        pe.wait_ge(all_lo[0], b + 2)
                    elif output:
                        pe.wait_ge(attention_copied, b)
                    elif project and g == G - 2:
                        pe.wait_ge(v_ready, b + 1)
                    elif project:
                        pe.wait_ge(q4_ready, s + 1)
                    else:
                        pe.wait_ge(normed, n)
                    for i in range(QT):
                        last = nc.tensor.transpose(ps_m[0][:, i * P:(i + 1) * P], ot[:, i * P:(i + 1) * P], ident)
                    last.then_inc(outputs_turned_ready, 1)

                def attention_turned():
                    pe.wait_ge(normed, 4 * b)
                    if project:
                        pe.wait_ge(q4_ready, s + 1)
                    for i in range(QT):
                        last = nc.tensor.transpose(ps_m[0][:, i * P:(i + 1) * P], attn[:, i, :], ident)
                    last.then_inc(attention_turned_ready, 1)

                def output_projected():
                    pe.wait_ge(attention_copied, b)
                    if projects_next(b):
                        pe.wait_ge(all_lo[1], b + 2)
                    elif project:
                        pe.wait_ge(k4_ready, s + 1)
                    else:
                        pe.wait_ge(xlo_ready[1], b - 1)
                    for i in range(QT):
                        last = mm(ps_m[1][:, i * P:(i + 1) * P], attn_t[:, i * P:(i + 1) * P], wo[:, :], start=True,
                                  stop=True)
                    last.then_inc(output_projected_ready, 1)

                def maxima_turned():
                    n, par = s - 2, g % 2
                    pe.wait_ge(maxima_found, NRED * (n + 1))
                    _, before_turned = normalisations(b, g - 1)
                    if g == 0 and early(b, g, 5):
                        pe.wait_ge(all_lo[1], 2)
                    elif g == 0:
                        pe.wait_ge(x2_ready, b - 1)
                    elif before_turned is not None:
                        pe.wait_ge(xlo_ready[before_turned], normalised(before_turned, b) + 1)
                    elif project:
                        pe.wait_ge(k4_ready, s)
                    else:
                        pe.wait_ge(qf_ready, n)
                    for i in range(QT):
                        last = mm(ps_m[1][:, i * P:(i + 1) * P], mt[:, par, i, :], identh[:, :], start=True, stop=True)
                    last.then_inc(maxima_turned_ready, 1)

                _, to_turn = normalisations(b, g)
                for what, u in PE_ORDER:
                    if what == "scores a" and maxima:
                        a_scores(u)
                    elif what == "scores b" and scores:
                        b_scores(u)
                    elif what == "q rows" and project:
                        project_q(b, g, s)
                    elif what == "k rows" and project:
                        project_k(b, g, s)
                    elif what == "q all" and projects_next(b) and g == G - 1:
                        pe.wait_ge(xlo_ready[0], b + 2)
                        pe.wait_ge(q4_ready, s + 1)
                        if output:
                            pe.wait_ge(attention_copied, b)
                        project_all(0, b + 1)
                    elif what == "k all" and projects_next(b) and g == G - 1:
                        pe.wait_ge(k4_ready, s + 1)
                        project_all(1, b + 1)
                    elif what == "v all" and project and g == G - 2:
                        project_v(b, s)
                    elif what == "values" and values:
                        weighted_values(u)
                    elif what == "outputs" and values:
                        outputs_turned()
                    elif what == "attention" and output:
                        attention_turned()
                    elif what == "projection" and output:
                        output_projected()
                    elif what == "maxima" and scores:
                        maxima_turned()
                    elif what == "x" and to_turn is not None:
                        if project:
                            pe.wait_ge(k4_ready, s + 1)
                        else:
                            pe.wait_ge(qf_ready, B * G)
                        turned(to_turn, normalised(to_turn, b))
                if isinstance(b, int) and s == B * G + 2:
                    pe.wait_ge(wu_low, 4)
                    pe.wait_ge(bias_split, 8)
                    pe.wait_ge(filled, 7)
                    pe.wait_ge(maxima_found, NRED * B * G)
                    pe.wait_ge(probs_ready, NU * B * G)
                    pe.wait_ge(ffn_prep, 4)
                    gate(0)
                    shared_up(0)

            blocks(pe, step)
            shared_up(1)
            ranks(0)
            turned(1, B - 1)
            shared_down(0, 0)
            pe.wait_ge(xlo_ready[1], B)
            pe.wait_ge(normed, B * G)
            gate(1)
            shared_up(2)
            pe.wait_ge(routed, 1)
            shared_down(1, 1)
            shared_up(3)
            ranks(1)
            shared_down(2, 0)
            with pe.Fori(2, B // 2) as m:
                shared_up(2 * m)
                shared_down(2 * m - 1, 1)
                shared_up(2 * m + 1)
                shared_down(2 * m, 0)
            shared_down(B - 1, 1)
            pe.wait_ge(table_ready, 1 + PARTS)

            def experts(jb):
                return numbers(jb, 0, NX + 1, mybir.EngineType.PE)

            def tile_mms(jb, k, e, h):
                j = NX * jb + k
                first = isinstance(jb, int) and jb == 0
                if not isinstance(jb, int) or j < NJ:
                    pe.wait_ge(xt_in[k], 16 * (jb + 1))
                    nc.tensor.transpose(ps_m[k % 2][:, 0:P], xt[:, k, 0:D], ident).then_inc(tile_turned, 1)
                if not isinstance(jb, int) or 0 <= j - 1 < NJ:
                    q = (k - 1) % 2
                    pe.wait_ge(tile_lo, j)
                    for f in range(FC):
                        dst = ps_a[q][:, f * P:(f + 1) * P]
                        ws = bass.ds(e[k + 1] * F + f * P, P)
                        mm(dst, wu_hi[:, ws], xh[:, q, :], start=True, stop=False)
                        mm(dst, wu_hi[:, ws], xl[:, q, :], start=False, stop=False)
                        last = mm(dst, wu_lo[:, ws], xh[:, q, :], start=False, stop=True)
                    last.then_inc(tile_up, 1)
                if not isinstance(jb, int) or 0 <= j - 2 < NJ:
                    q = k % 2
                    pe.wait_ge(tile_activated, j - 1)
                    if first and k == 2:
                        pe.wait_ge(shared_added_done, B)
                    if isinstance(jb, int) and j - 1 >= NJ:
                        pe.wait_ge(tile_output, j - 3)
                    for f in range(FC):
                        last = mm(ps_down[q][:, 0:D], act2[:, q, f, :], wd[:, bass.ds(e[k] * (FC * D) + f * D, D)],
                                  start=(f == 0), stop=(f == FC - 1))
                    last.then_inc(tile_down, 1)

            tile_blocks(pe, tile_mms, experts)


def kernel(L0_attn_x, L0_attn_w_qkv, L0_attn_w_o, L0_ffn_gate_w, L0_ffn_gate_bias, L0_ffn_Wu, L0_ffn_bu, L0_ffn_Wd,
           L0_ffn_bd, L0_ffn_sWu, L0_ffn_sbu, L0_ffn_sWd, L0_ffn_sbd):
    import numpy as np
    import concourse.bacc as bacc
    from concourse.bass_utils import run_bass_kernel_spmd

    a = {k: np.asarray(v) for k, v in locals().items() if k.startswith("L0_")}
    c = np.ascontiguousarray
    arrays = {
        "x": c(a["L0_attn_x"].reshape(T, D)),
        "wqkv": c(a["L0_attn_w_qkv"].reshape(3 * D, D).T),
        "wo": c(a["L0_attn_w_o"].T),
        "gate": c(a["L0_ffn_gate_w"].T),
        "gbias": c(a["L0_ffn_gate_bias"]),
        "wu": c(np.concatenate([a["L0_ffn_Wu"].reshape(E * F, D), a["L0_ffn_sWu"]]).T),
        "bu": c(a["L0_ffn_bu"].reshape(E, FC, P).transpose(2, 0, 1).reshape(P, E * FC)),
        "sbu": c(a["L0_ffn_sbu"].reshape(FC, P).T),
        "wd": c(np.concatenate([a["L0_ffn_Wd"], a["L0_ffn_sWd"][None]]).reshape(E + 1, D, FC, P)
                .transpose(3, 0, 2, 1).reshape(P, (E + 1) * FC * D)),
        "bd": c(np.concatenate([a["L0_ffn_bd"], a["L0_ffn_sbd"][None]]).reshape((E + 1) * D)),
        "const": constants(),
    }
    nc = bacc.Bacc("TRN2", target_bir_lowering=False, num_devices=1)
    aps = [nc.dram_tensor(f"in_{k}", v.shape, FP32, kind="ExternalInput").ap() for k, v in arrays.items()]
    out = nc.dram_tensor("out", (T, D), FP32, kind="ExternalOutput").ap()
    program(nc, *aps, out)
    r = run_bass_kernel_spmd(nc, [{f"in_{k}": v for k, v in arrays.items()}], core_ids=[0])
    return r.results[0]["out"].reshape(B, S, D)
```
